# Optimizing a Trainium2 kernel written in Bass

```python
import numpy as np
import jax
import jax.numpy as jnp

def _softmax(x, axis=-1):
    return jax.nn.softmax(x, axis=axis)

def _gelu(x):
    return jax.nn.gelu(x, approximate=True)

def _silu(x):
    return jax.nn.silu(x)

def _sigmoid(x):
    return jax.nn.sigmoid(x)

def _layernorm(x, axis=-1, eps=1e-05):
    m = jnp.mean(x, axis=axis, keepdims=True)
    v = jnp.var(x, axis=axis, keepdims=True)
    return (x - m) / jnp.sqrt(v + eps)

def _scatter_add(tgt, idx, src, axis=0):
    return tgt.at[idx].add(src)

def _segment_sum(src, seg, n):
    return jax.ops.segment_sum(src, seg, n)
kernel_name = 'mk_metaformer_d2_conv_nhwc512_r4_a82363'

def setup_inputs(seed: int=0):
    np.random.seed(seed)
    _w = jnp.asarray

    def _rec_inputs():
        import jax
        import jax.numpy as jnp
        _gk = jax.random.key(seed)
        x = -0.000125 + 0.9999 * jax.random.normal(jax.random.fold_in(_gk, 1), (16, 16, 16, 128), jnp.float32)
        return x
    x = _rec_inputs()

    def _L0_conv_setup():
        import jax, jax.numpy as jnp
        import numpy as np
        B, H, W, C = (16, 16, 16, 128)
        DIM, VDIM = (64, 64)
        key = jax.random.key(seed)
        ks = jax.random.split(key, 5)
        s = 0.02
        return {'x': jax.random.normal(ks[0], (B, H, W, C), jnp.float32), 'Wq': jax.random.normal(ks[1], (C, DIM), jnp.float32) * s, 'bq': jnp.zeros((DIM,), jnp.float32), 'Wk': jax.random.normal(ks[2], (C, VDIM), jnp.float32) * s, 'bk': jnp.zeros((VDIM,), jnp.float32), 'Wv': jax.random.normal(ks[3], (C, VDIM), jnp.float32) * s, 'bv': jnp.zeros((VDIM,), jnp.float32), 'Wr': jax.random.normal(ks[4], (DIM, C), jnp.float32) * s, 'br': jnp.zeros((C,), jnp.float32)}
    _L0_conv_all = _L0_conv_setup()
    _L0_conv_in = {k: v for k, v in _L0_conv_all.items() if k in ('Wq', 'bq', 'Wk', 'bk', 'Wv', 'bv', 'Wr', 'br')}
    del _L0_conv_all

    def _L0_ffn_setup():
        import jax, jax.numpy as jnp
        import numpy as np
        B, L, D, H, E, K = (8, 2048, 128, 512, 8, 2)
        SCALE = 0.02
        key = jax.random.key(seed)
        ks = jax.random.split(key, 6)
        return {'x': jax.random.normal(ks[0], (B, L, D), dtype=jnp.float32), 'Wg': jax.random.normal(ks[1], (D, E), dtype=jnp.float32) * SCALE, 'W1': jax.random.normal(ks[2], (E, D, H), dtype=jnp.float32) * SCALE, 'b1': jax.random.normal(ks[3], (E, H), dtype=jnp.float32) * SCALE, 'W2': jax.random.normal(ks[4], (E, H, D), dtype=jnp.float32) * SCALE, 'b2': jax.random.normal(ks[5], (E, D), dtype=jnp.float32) * SCALE}
    _L0_ffn_all = _L0_ffn_setup()
    _L0_ffn_in = {k: v for k, v in _L0_ffn_all.items() if k in ('Wg', 'W1', 'b1', 'W2', 'b2')}
    del _L0_ffn_all

    def _L1_conv_setup():
        import jax, jax.numpy as jnp
        import numpy as np
        from jax import lax
        B, H, W = (32, 16, 16)
        G, FI, FO, K = (8, 16, 16, 3)
        key = jax.random.key(seed)
        k1, k2 = jax.random.split(key)
        x = jax.random.normal(k1, (B, H, W, G * FI), dtype=jnp.float32)
        fan_in = K * K * FI
        kernel = jax.random.normal(k2, (K, K, FI, G * FO), dtype=jnp.float32) * np.sqrt(2.0 / fan_in).astype(np.float32)
        bias = jnp.zeros((G * FO,), dtype=jnp.float32)
        return {'x': x, 'kernel': kernel, 'bias': bias}
    _L1_conv_all = _L1_conv_setup()
    _L1_conv_in = {k: v for k, v in _L1_conv_all.items() if k in ('kernel', 'bias')}
    del _L1_conv_all

    def _L1_ffn_setup():
        import jax, jax.numpy as jnp
        import numpy as np
        STEP_SIZE = 0.1

        def _mlp(y, W1, b1, W2, b2, W3, b3):
            h = jnp.tanh(y @ W1.T + b1)
            h = jnp.tanh(h @ W2.T + b2)
            return h @ W3.T + b3

        def _rk4_step(y, dt, params):
            f = lambda z: _mlp(z, *params)
            k1 = f(y)
            k2 = f(y + dt / 2 * k1)
            k3 = f(y + dt / 2 * k2)
            k4 = f(y + dt * k3)
            return y + dt * (k1 + 2 * k2 + 2 * k3 + k4) / 6
        key = jax.random.key(seed)
        ks = jax.random.split(key, 7)
        B, S, D, H = (64, 16, 128, 512)
        return {'x': jax.random.normal(ks[0], (B, S, D), dtype=jnp.float32), 'W1': jax.random.normal(ks[1], (H, D), dtype=jnp.float32) * (1.0 / np.sqrt(D)), 'b1': jax.random.normal(ks[2], (H,), dtype=jnp.float32) * 0.01, 'W2': jax.random.normal(ks[3], (H, H), dtype=jnp.float32) * (1.0 / np.sqrt(H)), 'b2': jax.random.normal(ks[4], (H,), dtype=jnp.float32) * 0.01, 'W3': jax.random.normal(ks[5], (D, H), dtype=jnp.float32) * (1.0 / np.sqrt(H)), 'b3': jax.random.normal(ks[6], (D,), dtype=jnp.float32) * 0.01}
    _L1_ffn_all = _L1_ffn_setup()
    _L1_ffn_in = {k: v for k, v in _L1_ffn_all.items() if k in ('W1', 'b1', 'W2', 'b2', 'W3', 'b3')}
    del _L1_ffn_all
    return {'x': x, 'L0_conv_Wq': _L0_conv_in['Wq'], 'L0_conv_bq': _L0_conv_in['bq'], 'L0_conv_Wk': _L0_conv_in['Wk'], 'L0_conv_bk': _L0_conv_in['bk'], 'L0_conv_Wv': _L0_conv_in['Wv'], 'L0_conv_bv': _L0_conv_in['bv'], 'L0_conv_Wr': _L0_conv_in['Wr'], 'L0_conv_br': _L0_conv_in['br'], 'L0_ffn_Wg': _L0_ffn_in['Wg'], 'L0_ffn_W1': _L0_ffn_in['W1'], 'L0_ffn_b1': _L0_ffn_in['b1'], 'L0_ffn_W2': _L0_ffn_in['W2'], 'L0_ffn_b2': _L0_ffn_in['b2'], 'L1_conv_kernel': _L1_conv_in['kernel'], 'L1_conv_bias': _L1_conv_in['bias'], 'L1_ffn_W1': _L1_ffn_in['W1'], 'L1_ffn_b1': _L1_ffn_in['b1'], 'L1_ffn_W2': _L1_ffn_in['W2'], 'L1_ffn_b2': _L1_ffn_in['b2'], 'L1_ffn_W3': _L1_ffn_in['W3'], 'L1_ffn_b3': _L1_ffn_in['b3']}

def reference(x, L0_conv_Wq, L0_conv_bq, L0_conv_Wk, L0_conv_bk, L0_conv_Wv, L0_conv_bv, L0_conv_Wr, L0_conv_br, L0_ffn_Wg, L0_ffn_W1, L0_ffn_b1, L0_ffn_W2, L0_ffn_b2, L1_conv_kernel, L1_conv_bias, L1_ffn_W1, L1_ffn_b1, L1_ffn_W2, L1_ffn_b2, L1_ffn_W3, L1_ffn_b3):
    import jax
    import jax.numpy as jnp

    def _L0_conv_ref(x, Wq, bq, Wk, bk, Wv, bv, Wr, br):
        import jax, jax.numpy as jnp
        import numpy as np
        B, H, W, C = (16, 16, 16, 128)
        DIM, VDIM = (64, 64)
        b, h, w, c = x.shape
        n = h * w
        q = (x @ Wq + bq).reshape(b, n, -1)
        k = (x @ Wk + bk).reshape(b, n, -1)
        v = (x @ Wv + bv).reshape(b, n, -1)
        attention_maps = jax.nn.softmax(k, axis=1)
        attention_vectors = jax.nn.softmax(v, axis=1)
        global_descriptors = jnp.einsum('bnd,bnv->bvd', q, attention_maps)
        out = jnp.einsum('bvd,bnv->bnd', global_descriptors, attention_vectors)
        out = out.reshape(b, h, w, -1)
        return out @ Wr + br

    def _L0_ffn_ref(x, Wg, W1, b1, W2, b2):
        import jax, jax.numpy as jnp
        import numpy as np
        B, L, D, H, E, K = (8, 2048, 128, 512, 8, 2)
        SCALE = 0.02
        b, l, d = x.shape
        xt = x.reshape(-1, d)
        T = xt.shape[0]
        gate = jax.nn.softmax(xt @ Wg, axis=-1)
        topv, topi = jax.lax.top_k(gate, K)
        topv = topv / (jnp.sum(topv, axis=-1, keepdims=True) + 1e-06)
        scores = jnp.zeros((T, E), dtype=xt.dtype).at[jnp.arange(T)[:, None], topi].set(topv)
        out = jnp.zeros_like(xt)
        for e in range(E):
            h = jax.nn.gelu(xt @ W1[e] + b1[e], approximate=False)
            ye = h @ W2[e] + b2[e]
            out = out + ye * scores[:, e:e + 1]
        return out.reshape(b, l, d)

    def _L1_conv_ref(x, kernel, bias):
        import jax, jax.numpy as jnp
        import numpy as np
        from jax import lax
        B, H, W = (32, 16, 16)
        G, FI, FO, K = (8, 16, 16, 3)
        out = lax.conv_general_dilated(x, kernel, window_strides=(1, 1), padding='SAME', rhs_dilation=(1, 1), dimension_numbers=('NHWC', 'HWIO', 'NHWC'), feature_group_count=G)
        return out + bias

    def _L1_ffn_ref(x, W1, b1, W2, b2, W3, b3):
        import jax, jax.numpy as jnp
        import numpy as np
        STEP_SIZE = 0.1

        def _mlp(y, W1, b1, W2, b2, W3, b3):
            h = jnp.tanh(y @ W1.T + b1)
            h = jnp.tanh(h @ W2.T + b2)
            return h @ W3.T + b3

        def _rk4_step(y, dt, params):
            f = lambda z: _mlp(z, *params)
            k1 = f(y)
            k2 = f(y + dt / 2 * k1)
            k3 = f(y + dt / 2 * k2)
            k4 = f(y + dt * k3)
            return y + dt * (k1 + 2 * k2 + 2 * k3 + k4) / 6
        B, S, D = x.shape
        params = (W1, b1, W2, b2, W3, b3)
        span = 1.0 / (S - 1)
        steps = max(1, int(span / STEP_SIZE))
        dt = span / steps

        def interval(y, _):
            for _s in range(steps):
                y = _rk4_step(y, dt, params)
            return (y, y)
        y0 = x[:, 0]
        _, ys = jax.lax.scan(interval, y0, None, length=S - 1)
        return jnp.concatenate([y0[:, None], jnp.moveaxis(ys, 0, 1)], axis=1)

    def _gn(v, G=32, eps=1e-05):
        B_, H_, W_, C_ = v.shape
        g = v.reshape(B_, H_, W_, G, C_ // G)
        m = jnp.mean(g, axis=(1, 2, 4), keepdims=True)
        s = jnp.var(g, axis=(1, 2, 4), keepdims=True)
        return ((g - m) / jnp.sqrt(s + eps)).reshape(v.shape)

    def _ln_c(v, eps=1e-06):
        m = jnp.mean(v, axis=-1, keepdims=True)
        s = jnp.var(v, axis=-1, keepdims=True)
        return (v - m) / jnp.sqrt(s + eps)

    def _ln_t(v, eps=1e-05):
        m = jnp.mean(v, axis=-1, keepdims=True)
        s = jnp.var(v, axis=-1, keepdims=True)
        return (v - m) / jnp.sqrt(s + eps)

    def _to_tokens(v):
        B_, H_, W_, C_ = v.shape
        return v.reshape(B_, H_ * W_, C_)

    def _from_tokens(t, like):
        return t.reshape(like.shape)
    x = x + _L0_conv_ref(_ln_c(x), L0_conv_Wq, L0_conv_bq, L0_conv_Wk, L0_conv_bk, L0_conv_Wv, L0_conv_bv, L0_conv_Wr, L0_conv_br)
    t = _to_tokens(x)
    t = t + _L0_ffn_ref(_ln_t(t), L0_ffn_Wg, L0_ffn_W1, L0_ffn_b1, L0_ffn_W2, L0_ffn_b2)
    x = _from_tokens(t, x)
    x = x + _L1_conv_ref(_ln_c(x), L1_conv_kernel, L1_conv_bias)
    t = _to_tokens(x)
    t = t + _L1_ffn_ref(_ln_t(t), L1_ffn_W1, L1_ffn_b1, L1_ffn_W2, L1_ffn_b2, L1_ffn_W3, L1_ffn_b3)
    x = _from_tokens(t, x)
    return x

_drawn_inputs = setup_inputs


def setup_inputs(seed=0):
    import zlib

    import numpy as np

    out = dict(_drawn_inputs(seed))
    spreads = {'L0_conv_bq': (0.0, 0.8),
     'L0_conv_bk': (0.0, 2.0),
     'L0_conv_bv': (0.0, 2.0),
     'L0_conv_br': (0.0, 0.1),
     'L1_conv_bias': (0.0, 0.1)}
    factors = {'L0_conv_Wq': 8.0,
     'L0_conv_Wk': 8.0,
     'L0_conv_Wv': 8.0,
     'L0_conv_Wr': 8.0,
     'L0_ffn_b1': 8.0,
     'L0_ffn_b2': 3.578,
     'L1_ffn_b1': 41.986,
     'L1_ffn_b2': 26.396,
     'L1_ffn_b3': 8.0}
    for name, (base, spread) in spreads.items():
        noise = np.random.default_rng([zlib.crc32(name.encode()), seed]).standard_normal(out[name].shape)
        drawn = base * np.exp(spread * noise) if base else spread * noise
        out[name] = jnp.asarray(drawn.astype(out[name].dtype))
    for name, factor in factors.items():
        out[name] = (out[name] * factor).astype(out[name].dtype)
    return out
```

```python
from contextlib import ExitStack

import concourse.bass as bass
from concourse import mybir

F32 = mybir.dt.float32
F16 = mybir.dt.float16
BF16 = mybir.dt.bfloat16
ACT = mybir.ActivationFunctionType
ALU = mybir.AluOpType
AX = mybir.AxisListType

B, HW, C = 16, 16, 128
NPOS = HW * HW
TOK = B * NPOS
TILE = 512
IPT = TILE // NPOS
NT = TOK // TILE
PAIRS = NT // 2
QT = TILE // 128
DIM = 64
NE, HID = 8, 512
MC = HID // 128
TAPS = 9
PAD = HW + 2
STEPS = NPOS - 1
DT = 1.0 / STEPS
WSCALE = 256.0
NB = 2 * MC + 1
LN_CONV, LN_TOK = 1e-6, 1e-5


def build(nc, x, wkq, wv, wr, bkq, bv, br, wg, w1, b1, w2, b2, ck, cb, r1, r2, r3, rb, ident, iota, sel_e, sel_r, out):
    ctx = ExitStack()
    with ctx:
        def sb(name, shape, dt=F32):
            return ctx.enter_context(nc.sbuf_tensor(name, shape, dt))

        def sem(name):
            return ctx.enter_context(nc.semaphore(name))

        X = sb("X", [128, TOK])
        N = sb("N", [128, TOK])
        XT = sb("XT", [128, 2, QT, 128])
        ONES = sb("ONES", [128, 128])
        ID = sb("ID", [128, 128])
        D = sb("D", [128, 2, TILE])
        SQ = sb("SQ", [128, 2, TILE])
        SD = sb("SD", [128, 2, TILE])
        WKQ = sb("WKQ", [128, 128])
        WV = sb("WV", [128, DIM])
        WR = sb("WR", [DIM, 128])
        BKQ = sb("BKQ", [128, 1])
        BV = sb("BV", [DIM, 1])
        BR = sb("BR", [128, 1])
        KQ = sb("KQ", [128, 2, TILE])
        V = sb("V", [DIM, 2, TILE])
        TK = sb("TK", [128, 2, QT, 128])
        NM = sb("NM", [DIM, 2, 2 * IPT])
        SE = sb("SE", [DIM, 2, 2 * IPT])
        RP = sb("RP", [DIM, 2, IPT])
        GD = sb("GD", [DIM, 2, IPT, 128])
        OT = sb("OT", [DIM, 2, TILE])
        WG = sb("WG", [128, 128])
        LG = sb("LG", [128, 2, TILE])
        GP = sb("GP", [128, NT * QT, NE])
        GA = sb("GA", [128, NT * QT, NE])
        GO = sb("GO", [128, NT * QT, NE])
        GQ = sb("GQ", [128, NT * QT, NE])
        GR = sb("GR", [128, 8, NT * QT])
        IOTA = sb("IOTA", [128, NE])
        SS = sb("SS", [128, 2, QT, NE])
        ST = sb("ST", [NE, TOK])
        EPS = sb("EPS", [128, 2])
        SELE = sb("SELE", [NE, NE, 128])
        W1 = sb("W1", [128, NE, HID])
        B1 = sb("B1", [128, NE, MC])
        W2 = sb("W2", [128, NE, MC, 128])
        B2 = sb("B2", [NE, 128])
        G = sb("G", [128, 2, MC, TILE])
        CK = sb("CK", [128, TAPS, 128])
        CB = sb("CB", [128, 1])
        NP = sb("NP", [128, B, PAD, PAD])
        RH1, RL1 = sb("RH1", [128, MC, 128], F16), sb("RL1", [128, MC, 128], F16)
        RH2, RL2 = sb("RH2", [128, MC, MC, 128], F16), sb("RL2", [128, MC, MC, 128], F16)
        RH3, RL3 = sb("RH3", [128, MC, 128], F16), sb("RL3", [128, MC, 128], F16)
        RB = sb("RB", [NB, 5, 128])
        RBP = sb("RBP", [NB, 2, 128], BF16)
        BI = sb("BI", [128, 128], BF16)
        SELR = sb("SELR", [128, 3 * MC * B + B])
        SR = sb("SR", [128, 3 * MC * B + B], BF16)
        Z = sb("Z", [128, 2, B], F16)
        ZF = sb("ZF", [128, B])
        Y = sb("Y", [128, B])
        YA = sb("YA", [128, B])
        HA, HB = sb("HA", [128, MC, 2, B], F16), sb("HB", [128, MC, 2, B], F16)
        HAF, HBF = sb("HAF", [128, MC, B]), sb("HBF", [128, MC, B])
        HR = sb("HR", [128, MC, B])
        RW = G[:, :, :, :].rearrange("p a m n -> p (a m n)")
        R1F, R2F, R3F = RW[:, 0:512], RW[:, 512:2560], RW[:, 2560:3072]
        YS = N[:, :].rearrange("p (b s) -> p b s", b=B)

        PS = [ctx.enter_context(nc.psum_tensor(f"PS{i}", [128, 512], F32)) for i in range(8)]
        PA, PB = PS[0:2], PS[2:4]

        w_in = sem("w_in")
        x_in = [sem("x_in0"), sem("x_in1")]
        rk_in = sem("rk_in")
        ck_zero, ck_in = sem("ck_zero"), sem("ck_in")
        consts = sem("consts")
        x_tr, x_c = sem("x_tr"), sem("x_c")
        ln_mean, ln_dev, ln_sq, ln_var = sem("ln_mean"), sem("ln_dev"), sem("ln_sq"), sem("ln_var")
        ln_sd, ln_rec, ln_out = sem("ln_sd"), sem("ln_rec"), sem("ln_out")
        at_p, at_kqv, at_max, at_exp, at_tr = sem("at_p"), sem("at_kqv"), sem("at_max"), sem("at_exp"), sem("at_tr")
        at_prod, at_rp, at_tk, at_gd, at_gds = sem("at_prod"), sem("at_rp"), sem("at_tk"), sem("at_gd"), sem("at_gds")
        at_o, at_ot, at_y, at_x = sem("at_o"), sem("at_ot"), sem("at_y"), sem("at_x")
        g_l, g_lc, g_t, g_tc, g_v, g_e = sem("g_l"), sem("g_lc"), sem("g_t"), sem("g_tc"), sem("g_v"), sem("g_e")
        g_ss, g_st, g_sc = sem("g_ss"), sem("g_st"), sem("g_sc")
        mo_h, mo_g, mo_s, mo_d, mo_w, mo_acc, mo_x = (sem("mo_" + k) for k in ("h", "g", "s", "d", "w", "acc", "x"))
        np_zero, cv_y, cv_x = sem("np_zero"), sem("cv_y"), sem("cv_x")
        rk_split = sem("rk_split")
        rk_w, rk_z1, rk_zf, rk_z2, rk_y, rk_ya, rk_ys = (sem("rk_" + k) for k in ("w", "z1", "zf", "z2", "y", "ya", "ys"))
        rk_u, rk_a1, rk_af, rk_a2 = (sem("rk_" + k) for k in ("u", "a1", "af", "a2"))
        rk_v, rk_r, rk_b1, rk_bf, rk_b2, rk_k = (sem("rk_" + k) for k in ("v", "r", "b1", "bf", "b2", "k"))
        o_s, o_tr, o_c = sem("o_s"), sem("o_tr"), sem("o_c")
        o_out = [sem("o_out0"), sem("o_out1")]
        block = ctx.enter_context(nc.Block())

        def tile(i, par):
            return bass.ts(2 * i + par, TILE)

        def xblocks(dram, i, par):
            return dram[bass.ts(2 * i + par, TILE), :].rearrange("(q p) c -> p q c", p=128)

        WEIGHTS = [(ID[:, :], ident), (WKQ[:, :], wkq), (WV[:, :], wv), (WR[:, :], wr), (BKQ[:, :], bkq),
                   (BV[:, :], bv), (BR[:, :], br), (WG[:, 0:NE], wg), (B1[:, :, :], b1), (B2[:, :], b2),
                   (CB[:, :], cb), (IOTA[:, :], iota), (SELE[:, :, :], sel_e), (SELR[:, :], sel_r),
                   (RB[:, 0, :], rb), (W1[:, :, :], w1), (W2[:, :, :, :], w2), (R1F, r1), (R2F, r2), (R3F, r3)]

        @block.sync
        def _(sp):
            for par in range(2):
                sp.dma_start(XT[:, par], xblocks(x, 0, par)).then_inc(x_in[par], 16)
            sp.wait_ge(ck_zero, 2)
            for dst, src in WEIGHTS:
                sp.dma_start(dst, src).then_inc(w_in, 16)
            for g in range(8):
                sp.dma_start(CK[16 * g:16 * g + 16, :, 16 * g:16 * g + 16],
                             ck[:, :, 16 * g:16 * g + 16].rearrange("t i o -> i t o")).then_inc(ck_in, 16)
            with sp.Fori(1, PAIRS) as i:
                for par in range(2):
                    sp.wait_ge(x_c, 2 * i + par - 1)
                    sp.dma_start(XT[:, par], xblocks(x, i, par)).then_inc(x_in[par], 16)
            with sp.Fori(0, PAIRS) as i:
                for par in range(2):
                    sp.wait_ge(o_c, 2 * i + par + 1)
                    sp.dma_start(xblocks(out, i, par), XT[:, par]).then_inc(o_out[par], 16)
            for par in range(2):
                sp.wait_ge(o_out[par], 16 * PAIRS)

        @block.gpsimd
        def _(gp):
            nc.gpsimd.memset(WG[:, :], 0.0).then_inc(ck_zero, 1)
            nc.gpsimd.memset(CK[:, :, :], 0.0).then_inc(ck_zero, 1)
            nc.gpsimd.memset(NP[:, :, :, :], 0.0).then_inc(np_zero, 1)
            gp.wait_ge(rk_y, 1)
            nc.gpsimd.tensor_copy(YS[:, :, 0], Y[:, :]).then_inc(rk_ys, 1)
            with gp.Fori(0, STEPS) as s:
                gp.wait_ge(rk_y, s + 2)
                nc.gpsimd.tensor_copy(YS[:, :, bass.ds(s + 1, 1)], Y[:, :].unsqueeze(2)).then_inc(rk_ys, 1)

        @block.tensor
        def _(pe):
            mm = nc.tensor.matmul

            def layer_norm(p):
                with pe.Fori(0, PAIRS) as i:
                    for par in range(2):
                        if p == 0:
                            pe.wait_ge(x_c, 2 * i + par + 1)
                        mm(PA[par][:, :], ONES[:, :], X[:, tile(i, par)], start=True, stop=True).then_inc(ln_mean, 1)
                    for par in range(2):
                        pe.wait_ge(ln_sq, NT * p + 2 * i + par + 1)
                        mm(PB[par][:, :], ONES[:, :], SQ[:, par], start=True, stop=True).then_inc(ln_var, 1)

            pe.wait_ge(w_in, 16 * len(WEIGHTS))
            pe.wait_ge(consts, 1)
            with pe.Fori(0, PAIRS) as i:
                for par in range(2):
                    pe.wait_ge(x_in[par], 16 * i + 16)
                    for q in range(QT):
                        t = nc.tensor.transpose(PA[par][:, bass.ts(q, 128)], XT[:, par, q], ID[:, :])
                    t.then_inc(x_tr, 1)
            pe.wait_ge(x_c, NT)
            layer_norm(0)
            with pe.Fori(0, PAIRS) as i:
                for par in range(2):
                    pe.wait_ge(ln_out, 2 * i + par + 1)
                    if par == 0:
                        pe.wait_ge(ln_sd, NT)
                    mm(PA[par][:, :], WKQ[:, :], N[:, tile(i, par)], start=True, stop=True)
                    mm(PB[par][0:DIM, :], WV[:, :], N[:, tile(i, par)], start=True, stop=True).then_inc(at_p, 1)
                for par in range(2):
                    pe.wait_ge(at_exp, 2 * i + par + 1)
                    for q in range(QT):
                        t = nc.tensor.transpose(PA[par][:, bass.ts(q, 128)], KQ[:, par, bass.ts(q, 128)], ID[:, :])
                    t.then_inc(at_tr, 1)
                for par in range(2):
                    pe.wait_ge(at_tk, 2 * i + par + 1)
                    for b in range(IPT):
                        for h in range(2):
                            t = mm(PB[par][0:DIM, bass.ts(b, DIM)], TK[:, par, 2 * b + h, 0:DIM],
                                   TK[:, par, 2 * b + h, DIM:128], start=(h == 0), stop=(h == 1))
                    t.then_inc(at_gd, 1)
                for par in range(2):
                    pe.wait_ge(at_gds, 2 * i + par + 1)
                    for b in range(IPT):
                        t = mm(PA[par][:, bass.ts(b, NPOS)], GD[:, par, b], V[:, par, bass.ts(b, NPOS)],
                               start=True, stop=True)
                    t.then_inc(at_o, 1)
                for par in range(2):
                    pe.wait_ge(at_ot, 2 * i + par + 1)
                    mm(PB[par][:, :], WR[:, :], OT[:, par], start=True, stop=True).then_inc(at_y, 1)
                pe.wait_ge(at_x, 2 * i + 2)
            layer_norm(1)
            with pe.Fori(0, PAIRS) as i:
                for par in range(2):
                    pe.wait_ge(ln_out, NT + 2 * i + par + 1)
                    if par == 0:
                        pe.wait_ge(ln_sd, 2 * NT)
                    mm(PA[par][:, :], WG[:, :], N[:, tile(i, par)], start=True, stop=True).then_inc(g_l, 1)
                for par in range(2):
                    pe.wait_ge(g_lc, 2 * i + par + 1)
                    for q in range(QT):
                        t = nc.tensor.transpose(PB[par][:, bass.ts(q, 128)], LG[:, par, bass.ts(q, 128)], ID[:, :])
                    t.then_inc(g_t, 1)
                pe.wait_ge(g_tc, 2 * i + 2)
            with pe.Fori(0, PAIRS) as i:
                for par in range(2):
                    pe.wait_ge(g_ss, 2 * i + par + 1)
                    for q in range(QT):
                        t = nc.tensor.transpose(PA[par][0:NE, bass.ts(q, 128)], SS[:, par, q], ID[:, :])
                    t.then_inc(g_st, 1)
                pe.wait_ge(g_sc, 2 * i + 2)
            PH, PSC, PACC = PS[0:4], PS[4:6], PS[6]
            with pe.Fori(0, NT) as t:
                tok = bass.ts(t, TILE)
                mm(PACC[:, :], B2[:, :], ST[:, tok], start=True, stop=False)

                def down(e):
                    for m in range(MC):
                        pe.wait_ge(mo_d, t * (NE * MC) + e * MC + m + 1)
                        mm(PACC[:, :], W2[:, e, m], G[:, e % 2, m], start=False,
                           stop=(e == NE - 1 and m == MC - 1)).then_inc(mo_w, 1)

                for e in range(NE):
                    for m in range(MC):
                        if e:
                            pe.wait_ge(mo_g, t * (NE * MC) + (e - 1) * MC + m + 1)
                        mm(PH[m][:, :], W1[:, e, bass.ts(m, 128)], N[:, tok], start=True, stop=True).then_inc(mo_h, 1)
                    mm(PSC[e % 2][:, :], SELE[:, e], ST[:, tok], start=True, stop=True).then_inc(mo_s, 1)
                    if e:
                        down(e - 1)
                down(NE - 1)
                pe.wait_ge(mo_x, t + 1)
            layer_norm(2)
            pe.wait_ge(ck_in, 16 * 8)
            with pe.Fori(0, PAIRS) as i:
                for par in range(2):
                    pe.wait_ge(ln_out, 2 * NT + 2 * i + par + 1)
                    if par == 0:
                        pe.wait_ge(ln_sd, 3 * NT)
                    for tap in range(TAPS):
                        dy, dx = tap // 3, tap % 3
                        t = mm(PA[par][:, :], CK[:, tap], NP[:, bass.ts(2 * i + par, IPT), dy:dy + HW, dx:dx + HW],
                               start=(tap == 0), stop=(tap == TAPS - 1))
                    t.then_inc(cv_y, 1)
                pe.wait_ge(cv_x, 2 * i + 2)
            FIRST = X[:, :].rearrange("p (b s) -> p b s", b=B)[:, :, 0]
            mm(PA[0][:, 0:B], ONES[:, :], FIRST, start=True, stop=True).then_inc(ln_mean, 1)
            pe.wait_ge(ln_sq, 3 * NT + 1)
            mm(PB[0][:, 0:B], ONES[:, :], SQ[:, 0, 0:B], start=True, stop=True).then_inc(ln_var, 1)
            PU, PV, PK = PS[4:6], PS[6:8], PS[0]
            S1, S2, S3 = SR[:, 0:64], SR[:, 64:192], SR[:, 192:208]

            def bias_u():
                for h in range(2):
                    mm(PU[h][:, 0:2 * B], BI[:, :], S1[:, bass.ts(h, 2 * B)], start=True, stop=False)

            pe.wait_ge(rk_w, 1)
            pe.wait_ge(cv_x, NT)
            bias_u()
            with pe.Fori(0, STEPS) as s:
                for j in range(4):
                    def half(h):
                        return 8 * s + 2 * j + h + 1
                    pe.wait_ge(rk_z1, 4 * s + j + 1)
                    for m in range(MC):
                        o = PU[m // 2][:, bass.ts(m % 2, B)]
                        mm(o, RH1[:, m], Z[:, 0], start=False, stop=False)
                        mm(o, RL1[:, m], Z[:, 0], start=False, stop=False)
                    pe.wait_ge(rk_z2, 4 * s + j + 1)
                    for m in range(MC):
                        t = mm(PU[m // 2][:, bass.ts(m % 2, B)], RH1[:, m], Z[:, 1], start=False, stop=(m % 2 == 1))
                        if m % 2:
                            t.then_inc(rk_u, 1)
                    for h in range(2):
                        mm(PV[h][:, 0:4 * B], BI[:, :], S2[:, bass.ts(h, 4 * B)], start=True, stop=False)
                    for kh in range(2):
                        pe.wait_ge(rk_a1, half(kh))
                        for m in range(MC):
                            for k in (2 * kh, 2 * kh + 1):
                                mm(PV[m // 2][:, 2 * B * (m % 2):2 * B * (m % 2) + B], RL2[:, k, m], HA[:, k, 0],
                                   start=False, stop=False)
                    pe.wait_ge(rk_a2, half(1))
                    for k in range(2):
                        for m in range(MC):
                            mm(PV[m // 2][:, bass.ts(m % 2, 2 * B)], RH2[:, k, m], HA[:, k], start=False, stop=False)
                    for m in range(MC):
                        for k in (2, 3):
                            t = mm(PV[m // 2][:, bass.ts(m % 2, 2 * B)], RH2[:, k, m], HA[:, k], start=False,
                                   stop=(m % 2 == 1 and k == 3))
                        if m % 2:
                            t.then_inc(rk_v, 1)
                    mm(PK[:, 0:B], BI[:, :], S3, start=True, stop=False)
                    bias_u()
                    for kh in range(2):
                        pe.wait_ge(rk_b1, half(kh))
                        for k in (2 * kh, 2 * kh + 1):
                            mm(PK[:, 0:B], RH3[:, k], HB[:, k, 0], start=False, stop=False)
                            mm(PK[:, 0:B], RL3[:, k], HB[:, k, 0], start=False, stop=False)
                    pe.wait_ge(rk_b2, half(1))
                    for k in range(MC):
                        t = mm(PK[:, 0:B], RH3[:, k], HB[:, k, 1], start=False, stop=(k == MC - 1))
                    t.then_inc(rk_k, 1)
            for h in range(2):
                mm(PU[h][:, 0:2 * B], BI[:, :], S1[:, bass.ts(h, 2 * B)], start=False, stop=True)
            with pe.Fori(0, PAIRS) as i:
                for par in range(2):
                    pe.wait_ge(o_s, 2 * i + par + 1)
                    for q in range(QT):
                        t = nc.tensor.transpose(PS[2 + par][:, bass.ts(q, 128)], SQ[:, par, bass.ts(q, 128)], ID[:, :])
                    t.then_inc(o_tr, 1)
                pe.wait_ge(o_c, 2 * i + 2)

        @block.scalar
        def _(act):
            A = nc.scalar.activation

            def layer_norm(p, eps):
                with act.Fori(0, PAIRS) as i:
                    for par in range(2):
                        act.wait_ge(ln_dev, NT * p + 2 * i + par + 1)
                        A(SQ[:, par], D[:, par], ACT.Square).then_inc(ln_sq, 1)
                    for par in range(2):
                        act.wait_ge(ln_var, NT * p + 2 * i + par + 1)
                        A(SD[:, par], PB[par][:, :], ACT.Sqrt, bias=EPS[:, eps:eps + 1]).then_inc(ln_sd, 1)

            with act.Fori(0, PAIRS) as i:
                for par in range(2):
                    act.wait_ge(x_tr, 2 * i + par + 1)
                    nc.scalar.copy(X[:, tile(i, par)], PA[par][:, :]).then_inc(x_c, 1)
            act.wait_ge(consts, 1)
            layer_norm(0, 0)
            with act.Fori(0, PAIRS) as i:
                for par in range(2):
                    act.wait_ge(at_p, 2 * i + par + 1)
                    A(KQ[:, par], PA[par][:, :], ACT.Identity, bias=BKQ[:, :])
                    A(V[:, par], PB[par][0:DIM, :], ACT.Identity, bias=BV[:, :]).then_inc(at_kqv, 1)
                for par in range(2):
                    act.wait_ge(at_max, 2 * i + par + 1)
                    act.wait_ge(at_kqv, 2 * i + par + 1)
                    for b in range(IPT):
                        A(KQ[0:DIM, par, bass.ts(b, NPOS)], KQ[0:DIM, par, bass.ts(b, NPOS)], ACT.Exp,
                          bias=NM[:, par, b:b + 1], accum_out=SE[:, par, b:b + 1])
                        t = A(V[:, par, bass.ts(b, NPOS)], V[:, par, bass.ts(b, NPOS)], ACT.Exp,
                              bias=NM[:, par, IPT + b:IPT + b + 1], accum_out=SE[:, par, IPT + b:IPT + b + 1])
                    t.then_inc(at_exp, 1)
                for par in range(2):
                    act.wait_ge(at_tr, 2 * i + par + 1)
                    nc.scalar.copy(TK[:, par].rearrange("p q c -> p (q c)"), PA[par][:, :]).then_inc(at_tk, 1)
                for par in range(2):
                    act.wait_ge(at_o, 2 * i + par + 1)
                    nc.scalar.copy(OT[:, par], PA[par][0:DIM, :]).then_inc(at_ot, 1)
            layer_norm(1, 1)
            with act.Fori(0, PAIRS) as i:
                for par in range(2):
                    act.wait_ge(g_l, 2 * i + par + 1)
                    nc.scalar.copy(LG[:, par], PA[par][:, :]).then_inc(g_lc, 1)
            act.wait_ge(g_v, 2)
            A(GP[:, :, :], GA[:, :, :], ACT.Exp).then_inc(g_e, 1)
            with act.Fori(0, PAIRS) as i:
                for par in range(2):
                    act.wait_ge(g_st, 2 * i + par + 1)
                    nc.scalar.copy(ST[:, tile(i, par)], PA[par][0:NE, :]).then_inc(g_sc, 1)
            act.wait_ge(rk_w, 1)
            with act.Fori(0, NT) as t:
                for e in range(NE):
                    for m in range(MC):
                        act.wait_ge(mo_h, t * (NE * MC) + e * MC + m + 1)
                        if e >= 2:
                            act.wait_ge(mo_w, t * (NE * MC) + (e - 2) * MC + m + 1)
                        A(G[:, e % 2, m], PS[m][:, :], ACT.Gelu, bias=B1[:, e, m:m + 1]).then_inc(mo_g, 1)
                act.wait_ge(mo_w, t * (NE * MC) + NE * MC)
            layer_norm(2, 0)
            act.wait_ge(ln_dev, 3 * NT + 1)
            A(SQ[:, 0, 0:B], D[:, 0, 0:B], ACT.Square).then_inc(ln_sq, 1)
            act.wait_ge(ln_var, 3 * NT + 1)
            A(SD[:, 0, 0:B], PB[0][:, 0:B], ACT.Sqrt, bias=EPS[:, 1:2]).then_inc(ln_sd, 1)
            PU = PS[4:6]
            with act.Fori(0, STEPS) as s:
                for j in range(4):
                    for h in range(2):
                        act.wait_ge(rk_u, 8 * s + 2 * j + h + 1)
                        src = PU[h][:, 0:2 * B].rearrange("p (m b) -> p m b", m=2)
                        A(HA[:, 2 * h:2 * h + 2, 0], src, ACT.Tanh, scale=1.0 / WSCALE).then_inc(rk_a1, 1)
                        A(HAF[:, 2 * h:2 * h + 2], src, ACT.Tanh, scale=1.0 / WSCALE).then_inc(rk_af, 1)
                    for h in range(2):
                        act.wait_ge(rk_r, 8 * s + 2 * j + h + 1)
                        src = HR[:, 2 * h:2 * h + 2]
                        A(HB[:, 2 * h:2 * h + 2, 0], src, ACT.Tanh, scale=1.0 / WSCALE).then_inc(rk_b1, 1)
                        A(HBF[:, 2 * h:2 * h + 2], src, ACT.Tanh, scale=1.0 / WSCALE).then_inc(rk_bf, 1)
            with act.Fori(0, PAIRS) as i:
                for par in range(2):
                    act.wait_ge(o_tr, 2 * i + par + 1)
                    if par == 0:
                        act.wait_ge(o_out[0], 16 * i)
                        act.wait_ge(o_out[1], 16 * i)
                    nc.scalar.copy(XT[:, par].rearrange("p q c -> p (q c)"), PS[2 + par][:, :]).then_inc(o_c, 1)

        @block.vector
        def _(dve):
            v = nc.vector
            TT, TS, STT = v.tensor_tensor, v.tensor_scalar, v.scalar_tensor_tensor

            def layer_norm(p):
                with dve.Fori(0, PAIRS) as i:
                    for par in range(2):
                        dve.wait_ge(ln_mean, NT * p + 2 * i + par + 1)
                        TT(D[:, par], X[:, tile(i, par)], PA[par][:, :], ALU.subtract).then_inc(ln_dev, 1)
                    for par in range(2):
                        dve.wait_ge(ln_sd, NT * p + 2 * i + par + 1)
                        v.reciprocal(SD[:, par], SD[:, par]).then_inc(ln_rec, 1)
                    for par in range(2):
                        dve.wait_ge(ln_rec, NT * p + 2 * i + par + 1)
                        if p == 2:
                            dst = NP[:, bass.ts(2 * i + par, IPT), 1:HW + 1, 1:HW + 1]
                            TT(dst, D[:, par].rearrange("p (b y x) -> p b y x", b=IPT, y=HW),
                               SD[:, par].rearrange("p (b y x) -> p b y x", b=IPT, y=HW), ALU.mult).then_inc(ln_out, 1)
                        else:
                            TT(N[:, tile(i, par)], D[:, par], SD[:, par], ALU.mult).then_inc(ln_out, 1)
                    dve.wait_ge(ln_out, NT * p + 2 * i + 2)

            v.memset(EPS[:, 0:1], LN_CONV)
            v.memset(EPS[:, 1:2], LN_TOK)
            v.memset(BI[:, :], 0.0)
            v.memset(GD[:, :, :, :], 0.0)
            v.memset(ONES[:, :], 1.0 / C).then_inc(consts, 1)
            dve.wait_ge(w_in, 16 * len(WEIGHTS))
            dve.wait_ge(consts, 1)
            PARTS = [(RH1, RL1, R1F, "p m n -> p (m n)"), (RH2, RL2, R2F, "p k m n -> p (k m n)"),
                     (RH3, RL3, R3F, "p m n -> p (m n)")]
            for hi, _lo, src, flat in PARTS:
                TS(hi[:].rearrange(flat), src, WSCALE, None, ALU.mult).then_inc(rk_split, 1)
            dve.wait_ge(rk_split, 3)
            for hi, lo, src, flat in PARTS:
                STT(lo[:].rearrange(flat), src, WSCALE, hi[:].rearrange(flat), ALU.mult, ALU.subtract).then_inc(rk_split, 1)
            v.tensor_copy(SR[:, :], SELR[:, :]).then_inc(rk_split, 1)
            TS(RB[:, 1], RB[:, 0], WSCALE, None, ALU.mult).then_inc(rk_split, 1)
            dve.wait_ge(rk_split, 8)
            v.tensor_copy(BI[0:NB, :], RB[:, 1]).then_inc(rk_split, 1)
            dve.wait_ge(rk_split, 9)
            TT(RB[:, 2], RB[:, 1], BI[0:NB, :], ALU.subtract).then_inc(rk_split, 1)
            dve.wait_ge(rk_split, 10)
            v.tensor_copy(RBP[:, 0], RB[:, 2]).then_inc(rk_split, 1)
            dve.wait_ge(rk_split, 11)
            v.tensor_copy(BI[32:32 + NB, :], RBP[:, 0])
            TT(RB[:, 3], RB[:, 2], RBP[:, 0], ALU.subtract).then_inc(rk_split, 1)
            dve.wait_ge(rk_split, 12)
            v.tensor_copy(BI[64:64 + NB, :], RB[:, 3]).then_inc(rk_w, 1)

            layer_norm(0)
            with dve.Fori(0, PAIRS) as i:
                for par in range(2):
                    dve.wait_ge(at_kqv, 2 * i + par + 1)
                    v.tensor_reduce(NM[:, par, 0:IPT], KQ[0:DIM, par].rearrange("p (b n) -> p b n", b=IPT),
                                    AX.X, ALU.max, negate=True)
                    v.tensor_reduce(NM[:, par, IPT:2 * IPT], V[:, par].rearrange("p (b n) -> p b n", b=IPT),
                                    AX.X, ALU.max, negate=True).then_inc(at_max, 1)
                for par in range(2):
                    dve.wait_ge(at_exp, 2 * i + par + 1)
                    TT(RP[:, par], SE[:, par, 0:IPT], SE[:, par, IPT:2 * IPT], ALU.mult).then_inc(at_prod, 1)
                for par in range(2):
                    dve.wait_ge(at_prod, 2 * i + par + 1)
                    v.reciprocal(RP[:, par], RP[:, par]).then_inc(at_rp, 1)
                for par in range(2):
                    dve.wait_ge(at_rp, 2 * i + par + 1)
                    dve.wait_ge(at_gd, 2 * i + par + 1)
                    for b in range(IPT):
                        t = TS(GD[:, par, b, 0:DIM], PB[par][0:DIM, bass.ts(b, DIM)], RP[:, par, b:b + 1], None, ALU.mult)
                    t.then_inc(at_gds, 1)
                for par in range(2):
                    dve.wait_ge(at_y, 2 * i + par + 1)
                    STT(X[:, tile(i, par)], PB[par][:, :], BR[:, :], X[:, tile(i, par)], ALU.add, ALU.add).then_inc(at_x, 1)
            dve.wait_ge(at_x, NT)
            layer_norm(1)
            with dve.Fori(0, PAIRS) as i:
                for par in range(2):
                    dve.wait_ge(g_t, 2 * i + par + 1)
                    v.tensor_copy(GP[:, bass.ts(2 * i + par, QT)],
                                  PB[par][:, :].rearrange("p (q e) -> p q e", q=QT)[:, :, 0:NE]).then_inc(g_tc, 1)
            links = [0]

            def link(ins):
                links[0] += 1
                ins.then_inc(g_v, 1)
                dve.wait_ge(g_v, links[0])

            ALL = [128, NT * QT, NE]

            def wide(k):
                return GR[:, k].unsqueeze(2).to_broadcast(ALL)

            IO = IOTA[:, :].unsqueeze(1).to_broadcast(ALL)
            dve.wait_ge(g_tc, NT)
            link(v.tensor_reduce(GR[:, 0], GP[:, :, :], AX.X, ALU.max))
            link(TT(GA[:, :, :], GP[:, :, :], wide(0), ALU.subtract))
            dve.wait_ge(g_e, 1)
            link(v.tensor_reduce(GR[:, 1], GP[:, :, :], AX.X, ALU.add))
            link(v.reciprocal(GR[:, 1], GR[:, 1]))
            link(TT(GP[:, :, :], GP[:, :, :], wide(1), ALU.mult))
            link(v.tensor_reduce(GR[:, 2], GP[:, :, :], AX.X, ALU.max))
            link(TT(GA[:, :, :], GP[:, :, :], wide(2), ALU.is_lt))
            link(STT(GA[:, :, :], GA[:, :, :], float(NE), IO, ALU.mult, ALU.add))
            link(v.tensor_reduce(GR[:, 3], GA[:, :, :], AX.X, ALU.min))
            link(TT(GO[:, :, :], IO, wide(3), ALU.is_equal))
            link(STT(GQ[:, :, :], GO[:, :, :], -2.0, GP[:, :, :], ALU.mult, ALU.add))
            link(v.tensor_reduce(GR[:, 4], GQ[:, :, :], AX.X, ALU.max))
            link(TT(GA[:, :, :], GQ[:, :, :], wide(4), ALU.is_lt))
            link(STT(GA[:, :, :], GA[:, :, :], float(NE), IO, ALU.mult, ALU.add))
            link(v.tensor_reduce(GR[:, 5], GA[:, :, :], AX.X, ALU.min))
            link(TT(GQ[:, :, :], IO, wide(5), ALU.is_equal))
            link(TT(GO[:, :, :], GO[:, :, :], GQ[:, :, :], ALU.add))
            link(STT(GR[:, 6], GR[:, 2], 1e-6, GR[:, 4], ALU.add, ALU.add))
            link(v.reciprocal(GR[:, 6], GR[:, 6]))
            link(TT(GP[:, :, :], GP[:, :, :], GO[:, :, :], ALU.mult))
            link(TT(GP[:, :, :], GP[:, :, :], wide(6), ALU.mult))
            with dve.Fori(0, PAIRS) as i:
                for par in range(2):
                    v.tensor_copy(SS[:, par], GP[:, bass.ts(2 * i + par, QT)]).then_inc(g_ss, 1)
                dve.wait_ge(g_st, 2 * i + 2)
            with dve.Fori(0, NT) as t:
                for e in range(NE):
                    dve.wait_ge(mo_s, t * NE + e + 1)
                    for m in range(MC):
                        dve.wait_ge(mo_g, t * (NE * MC) + e * MC + m + 1)
                        TT(G[:, e % 2, m], G[:, e % 2, m], PS[4 + e % 2][:, :], ALU.mult).then_inc(mo_d, 1)
                dve.wait_ge(mo_w, t * (NE * MC) + NE * MC)
                TT(X[:, bass.ts(t, TILE)], X[:, bass.ts(t, TILE)], PS[6][:, :], ALU.add).then_inc(mo_x, 1)
            dve.wait_ge(mo_x, NT)
            dve.wait_ge(np_zero, 1)
            layer_norm(2)
            with dve.Fori(0, PAIRS) as i:
                for par in range(2):
                    dve.wait_ge(cv_y, 2 * i + par + 1)
                    STT(X[:, tile(i, par)], PA[par][:, :], CB[:, :], X[:, tile(i, par)], ALU.add, ALU.add).then_inc(cv_x, 1)
            dve.wait_ge(cv_x, NT)
            FIRST = X[:, :].rearrange("p (b s) -> p b s", b=B)[:, :, 0]
            dve.wait_ge(ln_mean, 3 * NT + 1)
            TT(D[:, 0, 0:B], FIRST, PA[0][:, 0:B], ALU.subtract).then_inc(ln_dev, 1)
            dve.wait_ge(ln_sd, 3 * NT + 1)
            v.reciprocal(SD[:, 0, 0:B], SD[:, 0, 0:B]).then_inc(ln_rec, 1)
            dve.wait_ge(ln_rec, 3 * NT + 1)
            TT(Z[:, 0], D[:, 0, 0:B], SD[:, 0, 0:B], ALU.mult).then_inc(rk_z1, 1)
            TT(Y[:, :], D[:, 0, 0:B], SD[:, 0, 0:B], ALU.mult).then_inc(rk_y, 1)
            dve.wait_ge(rk_y, 1)
            dve.wait_ge(rk_z1, 1)
            TT(Z[:, 1], Y[:, :], Z[:, 0], ALU.subtract).then_inc(rk_z2, 1)
            STAGE = [DT / 2, DT / 2, DT]
            WEIGHT = [DT / 6, DT / 3, DT / 3, DT / 6]
            PV, PK = PS[6:8], PS[0][:, 0:B]
            with dve.Fori(0, STEPS) as s:
                for j in range(4):
                    for h in range(2):
                        dve.wait_ge(rk_af, 8 * s + 2 * j + h + 1)
                        sl = slice(2 * h, 2 * h + 2)
                        TT(HA[:, sl, 1], HAF[:, sl], HA[:, sl, 0], ALU.subtract).then_inc(rk_a2, 1)
                    for h in range(2):
                        dve.wait_ge(rk_v, 8 * s + 2 * j + h + 1)
                        v.tensor_reduce(HR[:, 2 * h:2 * h + 2], PV[h][:, 0:4 * B].rearrange("p (m c b) -> p m b c", m=2, c=2),
                                        AX.X, ALU.add).then_inc(rk_r, 1)
                    for h in range(2):
                        dve.wait_ge(rk_bf, 8 * s + 2 * j + h + 1)
                        sl = slice(2 * h, 2 * h + 2)
                        TT(HB[:, sl, 1], HBF[:, sl], HB[:, sl, 0], ALU.subtract).then_inc(rk_b2, 1)
                    dve.wait_ge(rk_k, 4 * s + j + 1)
                    if j < 3:
                        STT(Z[:, 0], PK, STAGE[j] / WSCALE, Y[:, :], ALU.mult, ALU.add).then_inc(rk_z1, 1)
                        STT(ZF[:, :], PK, STAGE[j] / WSCALE, Y[:, :], ALU.mult, ALU.add).then_inc(rk_zf, 1)
                        dve.wait_ge(rk_zf, 3 * s + j + 1)
                        TT(Z[:, 1], ZF[:, :], Z[:, 0], ALU.subtract).then_inc(rk_z2, 1)
                        if j:
                            dve.wait_ge(rk_ya, 3 * s + j)
                        STT(YA[:, :], PK, WEIGHT[j] / WSCALE, (YA if j else Y)[:, :], ALU.mult, ALU.add).then_inc(rk_ya, 1)
                    else:
                        dve.wait_ge(rk_ya, 3 * s + 3)
                        STT(Z[:, 0], PK, WEIGHT[3] / WSCALE, YA[:, :], ALU.mult, ALU.add).then_inc(rk_z1, 1)
                        dve.wait_ge(rk_ys, s + 1)
                        STT(Y[:, :], PK, WEIGHT[3] / WSCALE, YA[:, :], ALU.mult, ALU.add).then_inc(rk_y, 1)
                        dve.wait_ge(rk_y, s + 2)
                        TT(Z[:, 1], Y[:, :], Z[:, 0], ALU.subtract).then_inc(rk_z2, 1)
            dve.wait_ge(rk_ys, STEPS + 1)
            with dve.Fori(0, PAIRS) as i:
                for par in range(2):
                    TT(SQ[:, par], X[:, tile(i, par)], N[:, tile(i, par)], ALU.add).then_inc(o_s, 1)
                dve.wait_ge(o_tr, 2 * i + 2)


def kernel(**inputs):
    import numpy as np
    import concourse.bacc as bacc
    from concourse.bass_utils import run_bass_kernel_spmd

    f = {k: np.asarray(a) for k, a in inputs.items()}
    t = np.ascontiguousarray
    sel_r = np.zeros((128, 3 * MC * B + B), np.float32)
    for part in range(3):
        for m in range(MC):
            sel_r[32 * part + m, m * B:(m + 1) * B] = 1
            sel_r[32 * part + MC + m, MC * B + 2 * m * B:MC * B + (2 * m + 1) * B] = 1
        sel_r[32 * part + 2 * MC, 3 * MC * B:] = 1
    sel_e = np.zeros((NE, NE, 128), np.float32)
    for e in range(NE):
        sel_e[e, e] = 1
    arrays = {
        "x": f["x"].reshape(TOK, C),
        "wkq": np.concatenate([f["L0_conv_Wk"], f["L0_conv_Wq"]], 1),
        "wv": f["L0_conv_Wv"], "wr": f["L0_conv_Wr"],
        "bkq": np.concatenate([f["L0_conv_bk"], f["L0_conv_bq"]])[:, None],
        "bv": f["L0_conv_bv"][:, None], "br": f["L0_conv_br"][:, None],
        "wg": f["L0_ffn_Wg"],
        "w1": f["L0_ffn_W1"].transpose(1, 0, 2),
        "b1": f["L0_ffn_b1"].reshape(NE, MC, 128).transpose(2, 0, 1),
        "w2": f["L0_ffn_W2"].reshape(NE, MC, 128, C).transpose(2, 0, 1, 3),
        "b2": f["L0_ffn_b2"],
        "ck": f["L1_conv_kernel"].reshape(TAPS, 16, 128), "cb": f["L1_conv_bias"][:, None],
        "r1": f["L1_ffn_W1"].T,
        "r2": f["L1_ffn_W2"].T.reshape(MC, 128, HID).transpose(1, 0, 2).reshape(128, MC * HID),
        "r3": f["L1_ffn_W3"].T.reshape(MC, 128, C).transpose(1, 0, 2).reshape(128, MC * C),
        "rb": np.concatenate([f["L1_ffn_b1"].reshape(MC, 128), f["L1_ffn_b2"].reshape(MC, 128), f["L1_ffn_b3"][None]]),
        "ident": np.eye(128, dtype=np.float32),
        "iota": np.tile(np.arange(NE, dtype=np.float32), (128, 1)),
        "sel_e": sel_e, "sel_r": sel_r,
    }
    nc = bacc.Bacc("TRN2", target_bir_lowering=False, num_devices=1)
    feed, args = {}, []
    for name, a in arrays.items():
        feed[f"in_{name}"] = t(a)
        args.append(nc.dram_tensor(f"in_{name}", a.shape, mybir.dt.from_np(a.dtype), kind="ExternalInput").ap())
    args.append(nc.dram_tensor("out", (TOK, C), F32, kind="ExternalOutput").ap())
    build(nc, *args)
    r = run_bass_kernel_spmd(nc, [feed], core_ids=[0])
    return r.results[0]["out"].reshape(B, HW, HW, C)
```

```python
from contextlib import ExitStack

import concourse.bass as bass
from concourse import mybir

F32 = mybir.dt.float32
F16 = mybir.dt.float16
BF16 = mybir.dt.bfloat16
ACT = mybir.ActivationFunctionType
ALU = mybir.AluOpType
AX = mybir.AxisListType

B, HW, C = 16, 16, 128
NPOS = HW * HW
TOK = B * NPOS
TILE = 512
IPT = TILE // NPOS
NT = TOK // TILE
PAIRS = NT // 2
QT = TILE // 128
DIM = 64
NE, HID = 8, 512
MC = HID // 128
TAPS = 9
PAD = HW + 2
STEPS = NPOS - 1
DT = 1.0 / STEPS
SUM = 4 * B
SCALE_V = 2.0 ** 8
SCALE_U = 2.0 ** 16
COEF = (DT / 2, DT, DT / 6)
COEF_OF = (0, 0, 1, 2)
LN_CONV, LN_TOK = 1e-6, 1e-5


def build(nc, x, wkq, wv, wr, bkq, bv, br, wg, w1, b1, w2, b2, ck, cb, r1, r2, r3, r3n, rb1, rb2, rb3, ident, iota, sel_e, out):
    ctx = ExitStack()
    with ctx:
        def sb(name, shape, dt=F32):
            return ctx.enter_context(nc.sbuf_tensor(name, shape, dt))

        def sem(name):
            return ctx.enter_context(nc.semaphore(name))

        X = sb("X", [128, TOK])
        N = sb("N", [128, TOK])
        XT = sb("XT", [128, 2, QT, 128])
        ONES = sb("ONES", [128, 128])
        ID = sb("ID", [128, 128])
        D = sb("D", [128, 2, TILE])
        SQ = sb("SQ", [128, 2, TILE])
        SD = sb("SD", [128, 2, TILE])
        WKQ = sb("WKQ", [128, 128])
        WV = sb("WV", [128, DIM])
        WR = sb("WR", [DIM, 128])
        BKQ = sb("BKQ", [128, 1])
        BV = sb("BV", [DIM, 1])
        BR = sb("BR", [128, 1])
        KQ = D
        V = sb("V", [DIM, 2, TILE])
        TK = SQ[:, :, :].rearrange("p a (q c) -> p a q c", q=QT)
        NM = sb("NM", [DIM, 2, 2 * IPT])
        SE = sb("SE", [DIM, 2, 2 * IPT])
        RP = sb("RP", [DIM, 2, IPT])
        GD = sb("GD", [DIM, 2, IPT, 128])
        OT = SD[0:DIM, :, :]
        WG = sb("WG", [128, 128])
        LG = SQ
        GP = sb("GP", [128, NT * QT, NE])
        GA = sb("GA", [128, NT * QT, NE])
        GO = sb("GO", [128, NT * QT, NE])
        GQ = sb("GQ", [128, NT * QT, NE])
        GR = sb("GR", [128, 8, NT * QT])
        IOTA = sb("IOTA", [128, NE])
        SS = sb("SS", [128, 2, QT, NE])
        ST = sb("ST", [NE, TOK])
        EPS = sb("EPS", [128, 2])
        SELE = sb("SELE", [NE, NE, 128])
        W1 = sb("W1", [128, NE, HID])
        B1 = sb("B1", [128, NE, MC])
        W2 = sb("W2", [128, NE, MC, 128])
        B2 = sb("B2", [NE, 128])
        G = sb("G", [128, 2, MC, TILE])
        CK = sb("CK", [128, TAPS, 128])
        CB = sb("CB", [128, 1])
        NP = sb("NP", [128, B, PAD, PAD])
        RH2, RL2 = sb("RH2", [128, MC, MC, 128], F16), sb("RL2", [128, MC, MC, 128], F16)
        RH3, RL3 = sb("RH3", [128, MC, 128], F16), sb("RL3", [128, MC, 128], F16)
        RHU = sb("RHU", [128, 3, MC, MC, 128], F16)
        RLU = sb("RLU", [128, 3, MC, MC, 128], F16)
        IDU, IDV = sb("IDU", [128, 128], BF16), sb("IDV", [128, 128], BF16)
        RB1, RB2 = sb("RB1", [128, MC]), sb("RB2", [128, MC])
        RB3, RB3D = sb("RB3", [128, 1]), sb("RB3D", [128, 1])
        G0 = sb("G0", [128, MC])
        CW = sb("CW", [128, MC, B])
        CI = sb("CI", [128, 4, MC, 2, B], F16)
        R1K = sb("R1K", [128, HID])
        UI = sb("UI", [128, MC, 2, B], F16)
        AI = sb("AI", [128, MC, 2, B], F16)
        US = sb("US", [128, MC * B])
        DA = sb("DA", [128, MC * B])
        E = sb("E", [128, MC * B])
        AF = sb("AF", [128, MC, B])
        Y = sb("Y", [128, B])
        YD = sb("YD", [128, B])
        HA, HB = sb("HA", [128, MC, 2, B], F16), sb("HB", [128, MC, 2, B], F16)
        FA = sb("FA", [128, MC, B])
        FB = sb("FB", [128, 4, MC, B])
        HS, HT, HQ = (sb(n, [128, MC, B]) for n in ("HS", "HT", "HQ"))
        HSS = sb("HSS", [128, MC, 2, B], F16)
        RW = G[:, :, :, :].rearrange("p a m n -> p (a m n)")
        R1F, R2F, R3F, R3N = RW[:, 0:512], RW[:, 512:2560], RW[:, 2560:3072], RW[:, 3072:3584]
        YS = N[:, :].rearrange("p (b s) -> p b s", b=B)

        PSUM = ctx.enter_context(nc.psum_tensor("PSUM", [128, 8, 512], F32))
        PS = [PSUM[:, i] for i in range(8)]
        PA, PB = PS[0:2], PS[2:4]

        w_in = sem("w_in")
        x_in = [sem("x_in0"), sem("x_in1")]
        rk_in = sem("rk_in")
        ck_zero, ck_in = sem("ck_zero"), sem("ck_in")
        consts = sem("consts")
        x_tr, x_c = sem("x_tr"), sem("x_c")
        ln_mean, ln_dev, ln_sq, ln_var = sem("ln_mean"), sem("ln_dev"), sem("ln_sq"), sem("ln_var")
        ln_sd, ln_rec, ln_out = sem("ln_sd"), sem("ln_rec"), sem("ln_out")
        at_p, at_kqv, at_max, at_exp, at_tr = sem("at_p"), sem("at_kqv"), sem("at_max"), sem("at_exp"), sem("at_tr")
        at_prod, at_rp, at_tk, at_gd, at_gds = sem("at_prod"), sem("at_rp"), sem("at_tk"), sem("at_gd"), sem("at_gds")
        at_o, at_ot, at_y, at_x = sem("at_o"), sem("at_ot"), sem("at_y"), sem("at_x")
        g_l, g_lc, g_t, g_tc, g_v, g_e = sem("g_l"), sem("g_lc"), sem("g_t"), sem("g_tc"), sem("g_v"), sem("g_e")
        g_ss, g_st, g_sc = sem("g_ss"), sem("g_st"), sem("g_sc")
        mo_h, mo_g, mo_s, mo_d, mo_w, mo_acc, mo_x = (sem("mo_" + k) for k in ("h", "g", "s", "d", "w", "acc", "x"))
        np_zero, cv_y, cv_x = sem("np_zero"), sem("cv_y"), sem("cv_x")
        rk_split, rk_13, rk_w = sem("rk_split"), sem("rk_13"), sem("rk_w")
        rk_p, rk_r, rk_hi, rk_f, rk_lo = (sem("rk_" + k) for k in ("p", "r", "hi", "f", "lo"))
        rk_ui, rk_ai, rk_uh, rk_u, rk_e, rk_u0 = (sem("rk_" + k) for k in ("ui", "ai", "uh", "u", "e", "u0"))
        rk_hr, rk_hs, rk_hq, rk_k, rk_yd, rk_y, rk_ys = (sem("rk_" + k) for k in ("hr", "hs", "hq", "k", "yd", "y", "ys"))
        o_s, o_tr, o_c = sem("o_s"), sem("o_tr"), sem("o_c")
        o_out = [sem("o_out0"), sem("o_out1")]
        block = ctx.enter_context(nc.Block())

        def tile(i, par):
            return bass.ts(2 * i + par, TILE)

        def xblocks(dram, i, par):
            return dram[bass.ts(2 * i + par, TILE), :].rearrange("(q p) c -> p q c", p=128)

        WEIGHTS = [(ID[:, :], ident), (WKQ[:, :], wkq), (WV[:, :], wv), (WR[:, :], wr), (BKQ[:, :], bkq),
                   (BV[:, :], bv), (BR[:, :], br), (WG[:, 0:NE], wg), (B1[:, :, :], b1), (B2[:, :], b2),
                   (CB[:, :], cb), (IOTA[:, :], iota), (SELE[:, :, :], sel_e), (RB1[:, :], rb1), (RB2[:, :], rb2),
                   (RB3[:, :], rb3), (W1[:, :, :], w1), (W2[:, :, :, :], w2), (R1F, r1), (R2F, r2), (R3F, r3), (R3N, r3n)]

        def count(s, j, layer, h):
            return 16 * s + 4 * j + 2 * layer + h + 1

        @block.sync
        def _(sp):
            for par in range(2):
                sp.dma_start(XT[:, par], xblocks(x, 0, par)).then_inc(x_in[par], 16)
            sp.wait_ge(ck_zero, 2)
            for dst, src in WEIGHTS:
                sp.dma_start(dst, src).then_inc(w_in, 16)
            for g in range(8):
                sp.dma_start(CK[16 * g:16 * g + 16, :, 16 * g:16 * g + 16],
                             ck[:, :, 16 * g:16 * g + 16].rearrange("t i o -> i t o")).then_inc(ck_in, 16)
            with sp.Fori(1, PAIRS) as i:
                for par in range(2):
                    sp.wait_ge(x_c, 2 * i + par - 1)
                    sp.dma_start(XT[:, par], xblocks(x, i, par)).then_inc(x_in[par], 16)
            with sp.Fori(0, PAIRS) as i:
                for par in range(2):
                    sp.wait_ge(o_c, 2 * i + par + 1)
                    sp.dma_start(xblocks(out, i, par), XT[:, par]).then_inc(o_out[par], 16)
            for par in range(2):
                sp.wait_ge(o_out[par], 16 * PAIRS)

        @block.gpsimd
        def _(gp):
            nc.gpsimd.memset(WG[:, :], 0.0).then_inc(ck_zero, 1)
            nc.gpsimd.memset(CK[:, :, :], 0.0).then_inc(ck_zero, 1)
            nc.gpsimd.memset(NP[:, :, :, :], 0.0).then_inc(np_zero, 1)
            gp.wait_ge(rk_y, 1)
            nc.gpsimd.tensor_copy(YS[:, :, 0], Y[:, :]).then_inc(rk_ys, 1)
            g = nc.gpsimd

            def stage_sum(s):
                gp.wait_ge(rk_f, count(s, 3, 1, 1))
                g.tensor_tensor(HS[:, :, :], FB[:, 0], FB[:, 3], ALU.add).then_inc(rk_hr, 1)
                g.tensor_tensor(HT[:, :, :], FB[:, 1], FB[:, 2], ALU.add).then_inc(rk_hr, 1)
                gp.wait_ge(rk_hr, 2 * s + 2)
                g.tensor_tensor(HS[:, :, :], HS[:, :, :], HT[:, :, :], ALU.add).then_inc(rk_hq, 1)
                gp.wait_ge(rk_hq, 3 * s + 1)
                g.tensor_tensor(HQ[:, :, :], HS[:, :, :], HT[:, :, :], ALU.add).then_inc(rk_hq, 1)
                g.tensor_tensor(HSS[:, :, 0], HS[:, :, :], HT[:, :, :], ALU.add).then_inc(rk_hq, 1)
                gp.wait_ge(rk_hq, 3 * s + 3)
                g.tensor_tensor(HSS[:, :, 1], HQ[:, :, :], HSS[:, :, 0], ALU.subtract).then_inc(rk_hs, 1)

            stage_sum(0)
            with gp.Fori(1, STEPS) as s:
                gp.wait_ge(rk_y, s + 1)
                g.tensor_copy(YS[:, :, bass.ds(s, 1)], Y[:, :].unsqueeze(2)).then_inc(rk_ys, 1)
                stage_sum(s)
            gp.wait_ge(rk_y, STEPS + 1)
            g.tensor_copy(YS[:, :, STEPS], Y[:, :]).then_inc(rk_ys, 1)

        @block.tensor
        def _(pe):
            mm = nc.tensor.matmul

            def layer_norm(p):
                with pe.Fori(0, PAIRS) as i:
                    for par in range(2):
                        if p == 0:
                            pe.wait_ge(x_c, 2 * i + par + 1)
                        mm(PA[par][:, :], ONES[:, :], X[:, tile(i, par)], start=True, stop=True).then_inc(ln_mean, 1)
                    for par in range(2):
                        pe.wait_ge(ln_sq, NT * p + 2 * i + par + 1)
                        mm(PB[par][:, :], ONES[:, :], SQ[:, par], start=True, stop=True).then_inc(ln_var, 1)

            pe.wait_ge(w_in, 16 * len(WEIGHTS))
            pe.wait_ge(consts, 1)
            with pe.Fori(0, PAIRS) as i:
                for par in range(2):
                    pe.wait_ge(x_in[par], 16 * i + 16)
                    for q in range(QT):
                        t = nc.tensor.transpose(PA[par][:, bass.ts(q, 128)], XT[:, par, q], ID[:, :])
                    t.then_inc(x_tr, 1)
            for k in range(MC):
                mm(PS[4 + k], R3N[:, bass.ts(k, 128)], R1F, start=True, stop=True)
            pe.wait_ge(x_c, NT)
            for m in range(MC):
                t = mm(PA[0][:, m:m + 1], R1F[:, bass.ts(m, 128)], RB3[:, :], start=(m == 0), stop=(m == MC - 1))
            t.then_inc(rk_13, 1)
            pe.wait_ge(rk_w, 1)
            layer_norm(0)
            with pe.Fori(0, PAIRS) as i:
                for par in range(2):
                    pe.wait_ge(ln_out, 2 * i + par + 1)
                    if par == 0:
                        pe.wait_ge(ln_out, NT)
                    mm(PA[par][:, :], WKQ[:, :], N[:, tile(i, par)], start=True, stop=True)
                    mm(PB[par][0:DIM, :], WV[:, :], N[:, tile(i, par)], start=True, stop=True).then_inc(at_p, 1)
                for par in range(2):
                    pe.wait_ge(at_exp, 2 * i + par + 1)
                    for q in range(QT):
                        t = nc.tensor.transpose(PA[par][:, bass.ts(q, 128)], KQ[:, par, bass.ts(q, 128)], ID[:, :])
                    t.then_inc(at_tr, 1)
                for par in range(2):
                    pe.wait_ge(at_tk, 2 * i + par + 1)
                    for b in range(IPT):
                        for h in range(2):
                            t = mm(PB[par][0:DIM, bass.ts(b, DIM)], TK[:, par, 2 * b + h, 0:DIM],
                                   TK[:, par, 2 * b + h, DIM:128], start=(h == 0), stop=(h == 1))
                    t.then_inc(at_gd, 1)
                for par in range(2):
                    pe.wait_ge(at_gds, 2 * i + par + 1)
                    for b in range(IPT):
                        t = mm(PA[par][:, bass.ts(b, NPOS)], GD[:, par, b], V[:, par, bass.ts(b, NPOS)],
                               start=True, stop=True)
                    t.then_inc(at_o, 1)
                for par in range(2):
                    pe.wait_ge(at_ot, 2 * i + par + 1)
                    mm(PB[par][:, :], WR[:, :], OT[:, par], start=True, stop=True).then_inc(at_y, 1)
                pe.wait_ge(at_x, 2 * i + 2)
            layer_norm(1)
            with pe.Fori(0, PAIRS) as i:
                for par in range(2):
                    pe.wait_ge(ln_out, NT + 2 * i + par + 1)
                    if par == 0:
                        pe.wait_ge(ln_out, 2 * NT)
                    mm(PA[par][:, :], WG[:, :], N[:, tile(i, par)], start=True, stop=True).then_inc(g_l, 1)
                for par in range(2):
                    pe.wait_ge(g_lc, 2 * i + par + 1)
                    for q in range(QT):
                        t = nc.tensor.transpose(PB[par][:, bass.ts(q, 128)], LG[:, par, bass.ts(q, 128)], ID[:, :])
                    t.then_inc(g_t, 1)
                pe.wait_ge(g_tc, 2 * i + 2)
            with pe.Fori(0, PAIRS) as i:
                for par in range(2):
                    pe.wait_ge(g_ss, 2 * i + par + 1)
                    for q in range(QT):
                        t = nc.tensor.transpose(PA[par][0:NE, bass.ts(q, 128)], SS[:, par, q], ID[:, :])
                    t.then_inc(g_st, 1)
                pe.wait_ge(g_sc, 2 * i + 2)
            PH, PSC, PACC = PS[0:4], PS[4:6], PS[6]
            with pe.Fori(0, NT) as t:
                tok = bass.ts(t, TILE)
                mm(PACC[:, :], B2[:, :], ST[:, tok], start=True, stop=False)

                def down(e):
                    for m in range(MC):
                        pe.wait_ge(mo_d, t * (NE * MC) + e * MC + m + 1)
                        mm(PACC[:, :], W2[:, e, m], G[:, e % 2, m], start=False,
                           stop=(e == NE - 1 and m == MC - 1)).then_inc(mo_w, 1)

                for e in range(NE):
                    for m in range(MC):
                        if e:
                            pe.wait_ge(mo_g, t * (NE * MC) + (e - 1) * MC + m + 1)
                        mm(PH[m][:, :], W1[:, e, bass.ts(m, 128)], N[:, tok], start=True, stop=True).then_inc(mo_h, 1)
                    mm(PSC[e % 2][:, :], SELE[:, e], ST[:, tok], start=True, stop=True).then_inc(mo_s, 1)
                    if e:
                        down(e - 1)
                down(NE - 1)
                pe.wait_ge(mo_x, t + 1)
            layer_norm(2)
            pe.wait_ge(ck_in, 16 * 8)
            with pe.Fori(0, PAIRS) as i:
                for par in range(2):
                    pe.wait_ge(ln_out, 2 * NT + 2 * i + par + 1)
                    if par == 0:
                        pe.wait_ge(ln_sd, 3 * NT)
                    for tap in range(TAPS):
                        dy, dx = tap // 3, tap % 3
                        t = mm(PA[par][:, :], CK[:, tap], NP[:, bass.ts(2 * i + par, IPT), dy:dy + HW, dx:dx + HW],
                               start=(tap == 0), stop=(tap == TAPS - 1))
                    t.then_inc(cv_y, 1)
                pe.wait_ge(cv_x, 2 * i + 2)
            FIRST = X[:, :].rearrange("p (b s) -> p b s", b=B)[:, :, 0]
            mm(PA[0][:, 0:B], ONES[:, :], FIRST, start=True, stop=True).then_inc(ln_mean, 1)
            pe.wait_ge(ln_sq, 3 * NT + 1)
            mm(PB[0][:, 0:B], ONES[:, :], SQ[:, 0, 0:B], start=True, stop=True).then_inc(ln_var, 1)
            pe.wait_ge(rk_y, 1)
            for m in range(MC):
                t = mm(PS[6][:, bass.ts(m, B)], R1K[:, bass.ts(m, 128)], Y[:, :], start=(m == 0), stop=(m == MC - 1))
            t.then_inc(rk_u0, 1)
            PP, PK = (PS[0:2], PS[2:4]), PS[4]
            W = 2 * 2 * B

            def inject(lay, ident, what, start):
                for h in range(2):
                    mm(PP[lay][h][:, 0:W], ident[:, :], what[:, 2 * h:2 * h + 2], start=start, stop=False)

            def layer(s, j, lay, hi, lo, src, late):
                out = PP[1 - lay]

                def low(ks, ms):
                    for m in ms:
                        for k in ks:
                            mm(out[m // 2][:, 2 * B * (m % 2):2 * B * (m % 2) + B], lo[:, k, m], src[:, k, 0],
                               start=False, stop=False)

                def high(ks, ms, stop):
                    for m in ms:
                        for k in ks:
                            t = mm(out[m // 2][:, bass.ts(m % 2, 2 * B)], hi[:, k, m], src[:, k], start=False,
                                   stop=(stop and m % 2 == 1 and k == 3))
                    return t

                pe.wait_ge(rk_hi, count(s, j, lay, 0))
                low((0, 1), range(MC))
                pe.wait_ge(rk_hi, count(s, j, lay, 1))
                low((2, 3), (0, 1))
                late()
                pe.wait_ge(rk_lo, count(s, j, lay, 0))
                high((0, 1), range(MC), False)
                pe.wait_ge(rk_lo, count(s, j, lay, 1))
                high((2, 3), (0, 1), True).then_inc(rk_p, 1)
                low((2, 3), (2, 3))
                high((2, 3), (2, 3), True).then_inc(rk_p, 1)

            def state_product():
                for k in range(MC):
                    mm(PK[:, 0:B], RH3[:, k], HSS[:, k, 0], start=(k == 0), stop=False)
                    mm(PK[:, 0:B], RL3[:, k], HSS[:, k, 0], start=False, stop=False)
                for k in range(MC):
                    t = mm(PK[:, 0:B], RH3[:, k], HSS[:, k, 1], start=False, stop=(k == MC - 1))
                t.then_inc(rk_k, 1)

            def step(s, first):
                for j in range(4):
                    inject(1, IDV, CI[:, 3], True)
                    layer(s, j, 0, RH2, RL2, HA, lambda: None)
                    pe.wait_ge(rk_u, 4 * s + j + 1)
                    inject(0, IDU, CI[:, COEF_OF[j]], True)
                    if j < 3:
                        if j == 0:
                            pe.wait_ge(rk_ui, s + 1)
                        inject(0, IDU, UI, False)
                    if j == 1 and not first:
                        pe.wait_ge(rk_hs, s)
                        state_product()

                    def late(j=j):
                        if j == 3:
                            pe.wait_ge(rk_ai, s + 2)
                            inject(0, IDU, AI, False)

                    layer(s, j, 1, RHU[:, COEF_OF[j]], RLU[:, COEF_OF[j]], HB, late)

            pe.wait_ge(rk_ai, 1)
            for h in range(2):
                mm(PP[0][h][:, 0:W], IDU[:, :], AI[:, 2 * h:2 * h + 2], start=True, stop=True).then_inc(rk_p, 1)
            step(0, True)
            with pe.Fori(1, STEPS) as s:
                step(s, False)
            pe.wait_ge(rk_hs, STEPS)
            state_product()
            with pe.Fori(0, PAIRS) as i:
                for par in range(2):
                    pe.wait_ge(o_s, 2 * i + par + 1)
                    for q in range(QT):
                        t = nc.tensor.transpose(PS[5 + par][:, bass.ts(q, 128)], SQ[:, par, bass.ts(q, 128)], ID[:, :])
                    t.then_inc(o_tr, 1)
                pe.wait_ge(o_c, 2 * i + 2)

        @block.scalar
        def _(act):
            A = nc.scalar.activation

            def layer_norm(p, eps):
                nc.scalar.preload_act_table_set("sqrt_and_others")
                with act.Fori(0, PAIRS) as i:
                    for par in range(2):
                        act.wait_ge(ln_dev, NT * p + 2 * i + par + 1)
                        A(SQ[:, par], D[:, par], ACT.Square).then_inc(ln_sq, 1)
                    for par in range(2):
                        act.wait_ge(ln_var, NT * p + 2 * i + par + 1)
                        A(SD[:, par], PB[par][:, :], ACT.Sqrt, bias=EPS[:, eps:eps + 1]).then_inc(ln_sd, 1)

            with act.Fori(0, PAIRS) as i:
                for par in range(2):
                    act.wait_ge(x_tr, 2 * i + par + 1)
                    nc.scalar.copy(X[:, tile(i, par)], PA[par][:, :]).then_inc(x_c, 1)
            act.wait_ge(consts, 1)
            layer_norm(0, 0)
            nc.scalar.preload_act_table_set("exp_and_others")
            with act.Fori(0, PAIRS) as i:
                for par in range(2):
                    act.wait_ge(at_p, 2 * i + par + 1)
                    A(KQ[:, par], PA[par][:, :], ACT.Identity, bias=BKQ[:, :])
                    A(V[:, par], PB[par][0:DIM, :], ACT.Identity, bias=BV[:, :]).then_inc(at_kqv, 1)
                for par in range(2):
                    act.wait_ge(at_max, 2 * i + par + 1)
                    act.wait_ge(at_kqv, 2 * i + par + 1)
                    for b in range(IPT):
                        A(KQ[0:DIM, par, bass.ts(b, NPOS)], KQ[0:DIM, par, bass.ts(b, NPOS)], ACT.Exp,
                          bias=NM[:, par, b:b + 1], accum_out=SE[:, par, b:b + 1])
                        t = A(V[:, par, bass.ts(b, NPOS)], V[:, par, bass.ts(b, NPOS)], ACT.Exp,
                              bias=NM[:, par, IPT + b:IPT + b + 1], accum_out=SE[:, par, IPT + b:IPT + b + 1])
                    t.then_inc(at_exp, 1)
                for par in range(2):
                    act.wait_ge(at_tr, 2 * i + par + 1)
                    nc.scalar.copy(TK[:, par].rearrange("p q c -> p (q c)"), PA[par][:, :]).then_inc(at_tk, 1)
                for par in range(2):
                    act.wait_ge(at_o, 2 * i + par + 1)
                    nc.scalar.copy(OT[:, par], PA[par][0:DIM, :]).then_inc(at_ot, 1)
            layer_norm(1, 1)
            with act.Fori(0, PAIRS) as i:
                for par in range(2):
                    act.wait_ge(g_l, 2 * i + par + 1)
                    nc.scalar.copy(LG[:, par], PA[par][:, :]).then_inc(g_lc, 1)
            act.wait_ge(g_v, 2)
            A(GP[:, :, :], GA[:, :, :], ACT.Exp).then_inc(g_e, 1)
            with act.Fori(0, PAIRS) as i:
                for par in range(2):
                    act.wait_ge(g_st, 2 * i + par + 1)
                    nc.scalar.copy(ST[:, tile(i, par)], PA[par][0:NE, :]).then_inc(g_sc, 1)
            nc.scalar.preload_act_table_set("gelu_and_others")
            act.wait_ge(rk_w, 1)
            with act.Fori(0, NT) as t:
                for e in range(NE):
                    for m in range(MC):
                        act.wait_ge(mo_h, t * (NE * MC) + e * MC + m + 1)
                        if e >= 2:
                            act.wait_ge(mo_w, t * (NE * MC) + (e - 2) * MC + m + 1)
                        A(G[:, e % 2, m], PS[m][:, :], ACT.Gelu, bias=B1[:, e, m:m + 1]).then_inc(mo_g, 1)
                act.wait_ge(mo_w, t * (NE * MC) + NE * MC)
            layer_norm(2, 0)
            act.wait_ge(ln_dev, 3 * NT + 1)
            A(SQ[:, 0, 0:B], D[:, 0, 0:B], ACT.Square).then_inc(ln_sq, 1)
            act.wait_ge(ln_var, 3 * NT + 1)
            A(SD[:, 0, 0:B], PB[0][:, 0:B], ACT.Sqrt, bias=EPS[:, 1:2]).then_inc(ln_sd, 1)
            nc.scalar.preload_act_table_set("gelu_and_others")

            def step(s, first):
                for j in range(4):
                    for lay, hi, f, scale in ((0, HA, FA, SCALE_U), (1, HB, FB[:, j], SCALE_V)):
                        if j == 0 and lay == 1 and not first:
                            act.wait_ge(rk_hr, 2 * s)
                        for h in range(2):
                            act.wait_ge(rk_r, count(s, j, lay, h))
                            src = PSUM[:, 2 * lay + h, SUM:SUM + 2 * B].rearrange("p (m b) -> p m b", m=2)
                            A(hi[:, 2 * h:2 * h + 2, 0], src, ACT.Tanh, scale=1.0 / scale).then_inc(rk_hi, 1)
                            A(f[:, 2 * h:2 * h + 2], src, ACT.Tanh, scale=1.0 / scale).then_inc(rk_f, 1)

            step(0, True)
            with act.Fori(1, STEPS) as s:
                step(s, False)
            with act.Fori(0, PAIRS) as i:
                for par in range(2):
                    act.wait_ge(o_tr, 2 * i + par + 1)
                    nc.scalar.copy(XT[:, par].rearrange("p q c -> p (q c)"), PS[5 + par][:, :]).then_inc(o_c, 1)
                act.wait_ge(o_out[0], 16 * i + 16)
                act.wait_ge(o_out[1], 16 * i + 16)

        @block.vector
        def _(dve):
            v = nc.vector
            TT, TS, STT = v.tensor_tensor, v.tensor_scalar, v.scalar_tensor_tensor

            def layer_norm(p):
                with dve.Fori(0, PAIRS) as i:
                    for par in range(2):
                        dve.wait_ge(ln_mean, NT * p + 2 * i + par + 1)
                        TT(D[:, par], X[:, tile(i, par)], PA[par][:, :], ALU.subtract).then_inc(ln_dev, 1)
                    for par in range(2):
                        dve.wait_ge(ln_sd, NT * p + 2 * i + par + 1)
                        v.reciprocal(SD[:, par], SD[:, par]).then_inc(ln_rec, 1)
                    for par in range(2):
                        dve.wait_ge(ln_rec, NT * p + 2 * i + par + 1)
                        if p == 2:
                            dst = NP[:, bass.ts(2 * i + par, IPT), 1:HW + 1, 1:HW + 1]
                            TT(dst, D[:, par].rearrange("p (b y x) -> p b y x", b=IPT, y=HW),
                               SD[:, par].rearrange("p (b y x) -> p b y x", b=IPT, y=HW), ALU.mult).then_inc(ln_out, 1)
                        else:
                            TT(N[:, tile(i, par)], D[:, par], SD[:, par], ALU.mult).then_inc(ln_out, 1)
                    dve.wait_ge(ln_out, NT * p + 2 * i + 2)

            v.memset(EPS[:, 0:1], LN_CONV)
            v.memset(EPS[:, 1:2], LN_TOK)
            v.memset(GD[:, :, :, :], 0.0)
            v.memset(ONES[:, :], 1.0 / C).then_inc(consts, 1)
            dve.wait_ge(w_in, 16 * len(WEIGHTS))
            dve.wait_ge(consts, 1)
            flat2, flat3 = "p k m n -> p (k m n)", "p m n -> p (m n)"
            PARTS = [(RH2[:].rearrange(flat2), RL2[:].rearrange(flat2), R2F, SCALE_V),
                     (RH3[:].rearrange(flat3), RL3[:].rearrange(flat3), R3F, SCALE_V)]
            dve.wait_ge(rk_13, 1)
            for c in range(3):
                PARTS.append((RHU[:, c], RLU[:, c], PSUM[:, 4:8].rearrange("p k (m n) -> p k m n", m=MC), SCALE_U * COEF[c]))
            for hi, _lo, src, scale in PARTS:
                TS(hi, src, scale, None, ALU.mult).then_inc(rk_split, 1)
            dve.wait_ge(rk_split, 5)
            for hi, lo, src, scale in PARTS:
                for k in range(MC) if len(lo.shape) == 4 else (slice(None),):
                    STT(lo[:, k], src[:, k], scale, hi[:, k], ALU.mult, ALU.subtract)
            v.tensor_copy(R1K[:, :], R1F)
            TS(IDU[:, :], ID[:, :], SCALE_U, None, ALU.mult)
            TS(IDV[:, :], ID[:, :], SCALE_V, None, ALU.mult)
            TS(RB3D[:, :], RB3[:, :], DT, None, ALU.mult)
            v.tensor_copy(G0[:, :], PA[0][:, 0:MC]).then_inc(rk_split, 1)
            dve.wait_ge(rk_split, 6)
            for n in range(4):
                src = (G0 if n < 3 else RB2)[:, :].unsqueeze(2).to_broadcast([128, MC, B])
                TS(CW[:, :, :], src, COEF[n] if n < 3 else 1.0, None, ALU.mult).then_inc(rk_split, 1)
                dve.wait_ge(rk_split, 7 + 3 * n)
                v.tensor_copy(CI[:, n, :, 0], CW[:, :, :]).then_inc(rk_split, 1)
                dve.wait_ge(rk_split, 8 + 3 * n)
                TT(CI[:, n, :, 1], CW[:, :, :], CI[:, n, :, 0], ALU.subtract).then_inc(rk_split, 1)
                dve.wait_ge(rk_split, 9 + 3 * n)
            v.memset(YD[:, :], 0.0).then_inc(rk_w, 1)

            layer_norm(0)
            with dve.Fori(0, PAIRS) as i:
                for par in range(2):
                    dve.wait_ge(at_kqv, 2 * i + par + 1)
                    v.tensor_reduce(NM[:, par, 0:IPT], KQ[0:DIM, par].rearrange("p (b n) -> p b n", b=IPT),
                                    AX.X, ALU.max, negate=True)
                    v.tensor_reduce(NM[:, par, IPT:2 * IPT], V[:, par].rearrange("p (b n) -> p b n", b=IPT),
                                    AX.X, ALU.max, negate=True).then_inc(at_max, 1)
                for par in range(2):
                    dve.wait_ge(at_exp, 2 * i + par + 1)
                    TT(RP[:, par], SE[:, par, 0:IPT], SE[:, par, IPT:2 * IPT], ALU.mult).then_inc(at_prod, 1)
                for par in range(2):
                    dve.wait_ge(at_prod, 2 * i + par + 1)
                    v.reciprocal(RP[:, par], RP[:, par]).then_inc(at_rp, 1)
                for par in range(2):
                    dve.wait_ge(at_rp, 2 * i + par + 1)
                    dve.wait_ge(at_gd, 2 * i + par + 1)
                    for b in range(IPT):
                        t = TS(GD[:, par, b, 0:DIM], PB[par][0:DIM, bass.ts(b, DIM)], RP[:, par, b:b + 1], None, ALU.mult)
                    t.then_inc(at_gds, 1)
                for par in range(2):
                    dve.wait_ge(at_y, 2 * i + par + 1)
                    STT(X[:, tile(i, par)], PB[par][:, :], BR[:, :], X[:, tile(i, par)], ALU.add, ALU.add).then_inc(at_x, 1)
            dve.wait_ge(at_x, NT)
            layer_norm(1)
            with dve.Fori(0, PAIRS) as i:
                for par in range(2):
                    dve.wait_ge(g_t, 2 * i + par + 1)
                    v.tensor_copy(GP[:, bass.ts(2 * i + par, QT)],
                                  PB[par][:, :].rearrange("p (q e) -> p q e", q=QT)[:, :, 0:NE]).then_inc(g_tc, 1)
            links = [0]

            def link(ins):
                links[0] += 1
                ins.then_inc(g_v, 1)
                dve.wait_ge(g_v, links[0])

            ALL = [128, NT * QT, NE]

            def wide(k):
                return GR[:, k].unsqueeze(2).to_broadcast(ALL)

            IO = IOTA[:, :].unsqueeze(1).to_broadcast(ALL)
            dve.wait_ge(g_tc, NT)
            link(v.tensor_reduce(GR[:, 0], GP[:, :, :], AX.X, ALU.max))
            link(TT(GA[:, :, :], GP[:, :, :], wide(0), ALU.subtract))
            dve.wait_ge(g_e, 1)
            link(v.tensor_reduce(GR[:, 1], GP[:, :, :], AX.X, ALU.add))
            link(v.reciprocal(GR[:, 1], GR[:, 1]))
            link(TT(GP[:, :, :], GP[:, :, :], wide(1), ALU.mult))
            link(v.tensor_reduce(GR[:, 2], GP[:, :, :], AX.X, ALU.max))
            link(TT(GA[:, :, :], GP[:, :, :], wide(2), ALU.is_lt))
            link(STT(GA[:, :, :], GA[:, :, :], float(NE), IO, ALU.mult, ALU.add))
            link(v.tensor_reduce(GR[:, 3], GA[:, :, :], AX.X, ALU.min))
            link(TT(GO[:, :, :], IO, wide(3), ALU.is_equal))
            link(STT(GQ[:, :, :], GO[:, :, :], -2.0, GP[:, :, :], ALU.mult, ALU.add))
            link(v.tensor_reduce(GR[:, 4], GQ[:, :, :], AX.X, ALU.max))
            link(TT(GA[:, :, :], GQ[:, :, :], wide(4), ALU.is_lt))
            link(STT(GA[:, :, :], GA[:, :, :], float(NE), IO, ALU.mult, ALU.add))
            link(v.tensor_reduce(GR[:, 5], GA[:, :, :], AX.X, ALU.min))
            link(TT(GQ[:, :, :], IO, wide(5), ALU.is_equal))
            link(TT(GO[:, :, :], GO[:, :, :], GQ[:, :, :], ALU.add))
            link(STT(GR[:, 6], GR[:, 2], 1e-6, GR[:, 4], ALU.add, ALU.add))
            link(v.reciprocal(GR[:, 6], GR[:, 6]))
            link(TT(GP[:, :, :], GP[:, :, :], GO[:, :, :], ALU.mult))
            link(TT(GP[:, :, :], GP[:, :, :], wide(6), ALU.mult))
            with dve.Fori(0, PAIRS) as i:
                for par in range(2):
                    v.tensor_copy(SS[:, par], GP[:, bass.ts(2 * i + par, QT)]).then_inc(g_ss, 1)
                dve.wait_ge(g_st, 2 * i + 2)
            with dve.Fori(0, NT) as t:
                for e in range(NE):
                    dve.wait_ge(mo_s, t * NE + e + 1)
                    for m in range(MC):
                        dve.wait_ge(mo_g, t * (NE * MC) + e * MC + m + 1)
                        TT(G[:, e % 2, m], G[:, e % 2, m], PS[4 + e % 2][:, :], ALU.mult).then_inc(mo_d, 1)
                dve.wait_ge(mo_w, t * (NE * MC) + NE * MC)
                TT(X[:, bass.ts(t, TILE)], X[:, bass.ts(t, TILE)], PS[6][:, :], ALU.add).then_inc(mo_x, 1)
            dve.wait_ge(mo_x, NT)
            dve.wait_ge(np_zero, 1)
            layer_norm(2)
            with dve.Fori(0, PAIRS) as i:
                for par in range(2):
                    dve.wait_ge(cv_y, 2 * i + par + 1)
                    STT(X[:, tile(i, par)], PA[par][:, :], CB[:, :], X[:, tile(i, par)], ALU.add, ALU.add).then_inc(cv_x, 1)
            dve.wait_ge(cv_x, NT)
            FIRST = X[:, :].rearrange("p (b s) -> p b s", b=B)[:, :, 0]
            dve.wait_ge(ln_mean, 3 * NT + 1)
            TT(D[:, 0, 0:B], FIRST, PA[0][:, 0:B], ALU.subtract).then_inc(ln_dev, 1)
            dve.wait_ge(ln_sd, 3 * NT + 1)
            v.reciprocal(SD[:, 0, 0:B], SD[:, 0, 0:B]).then_inc(ln_rec, 1)
            dve.wait_ge(ln_rec, 3 * NT + 1)
            TT(Y[:, :], D[:, 0, 0:B], SD[:, 0, 0:B], ALU.mult).then_inc(rk_y, 1)
            dve.wait_ge(rk_u0, 1)
            TT(US[:, :].rearrange("p (m b) -> p m b", m=MC), PS[6][:, 0:MC * B].rearrange("p (m b) -> p m b", m=MC),
               RB1[:, :].unsqueeze(2).to_broadcast([128, MC, B]), ALU.add).then_inc(rk_split, 1)
            dve.wait_ge(rk_split, 19)
            US3 = US[:, :].rearrange("p (m b) -> p m b", m=MC)
            v.tensor_copy(AI[:, :, 0], US3).then_inc(rk_split, 1)
            dve.wait_ge(rk_split, 20)
            TT(AI[:, :, 1], US3, AI[:, :, 0], ALU.subtract).then_inc(rk_ai, 1)
            BOTH = PSUM[:, 0:2, SUM:SUM + 2 * B]

            def two(a):
                return a[:, :].rearrange("p (h n) -> p h n", h=2)

            def step(s, first):
                for j in range(4):
                    for lay, hi, f in ((0, HA, FA), (1, HB, FB[:, j])):
                        for h in range(2):
                            bank = PSUM[:, 2 * lay + h]
                            dve.wait_ge(rk_p, count(s, j, lay, h))
                            v.tensor_reduce(bank[:, SUM:SUM + 2 * B].rearrange("p (m b) -> p m b", m=2),
                                            bank[:, 0:4 * B].rearrange("p (m c b) -> p m b c", m=2, c=2),
                                            AX.X, ALU.add).then_inc(rk_r, 1)
                        if lay == 1 and j == 3:
                            dve.wait_ge(rk_u, 4 * s + 4)
                            TT(AI[:, :, 1], AF[:, :, :], AI[:, :, 0], ALU.subtract).then_inc(rk_ai, 1)
                        for h in range(2):
                            dve.wait_ge(rk_f, count(s, j, lay, h))
                            sl = slice(2 * h, 2 * h + 2)
                            TT(hi[:, sl, 1], f[:, sl], hi[:, sl, 0], ALU.subtract).then_inc(rk_lo, 1)
                        if lay == 0:
                            if j == 0:
                                for h in range(2):
                                    TS(UI[:, 2 * h:2 * h + 2, 0], BOTH[:, h].rearrange("p (m b) -> p m b", m=2), 1.0 / SCALE_U, None,
                                       ALU.mult).then_inc(rk_uh, 1)
                                TS(two(US), BOTH, 1.0 / SCALE_U, None, ALU.mult).then_inc(rk_u, 1)
                                dve.wait_ge(rk_uh, 2 * s + 2)
                                dve.wait_ge(rk_u, 4 * s + 1)
                                TT(UI[:, :, 1], US3, UI[:, :, 0], ALU.subtract).then_inc(rk_ui, 1)
                            elif j == 1:
                                STT(two(DA), two(US), -4.0 * SCALE_U, BOTH, ALU.mult, ALU.add).then_inc(rk_u, 1)
                            elif j == 2:
                                dve.wait_ge(rk_u, 4 * s + 2)
                                STT(two(DA), BOTH, 2.0, two(DA), ALU.mult, ALU.add).then_inc(rk_u, 1)
                            else:
                                dve.wait_ge(rk_e, s + 1)
                                for h in range(2):
                                    b2 = BOTH[:, h].rearrange("p (m b) -> p m b", m=2)
                                    e2 = E[:, bass.ts(h, 2 * B)].rearrange("p (m b) -> p m b", m=2)
                                    STT(AI[:, 2 * h:2 * h + 2, 0], b2, 1.0 / 3.0 / SCALE_U, e2, ALU.mult, ALU.add)
                                STT(AF[:, :, :].rearrange("p (h m) b -> p h (m b)", h=2), BOTH, 1.0 / 3.0 / SCALE_U, two(E),
                                    ALU.mult, ALU.add).then_inc(rk_u, 1)
                        if lay == 1 and j == 2:
                            STT(E[:, :], DA[:, :], 1.0 / 3.0 / SCALE_U, US[:, :], ALU.mult, ALU.add).then_inc(rk_e, 1)
                            if not first:
                                state(s)

            def state(s):
                dve.wait_ge(rk_k, s)
                TS(YD[:, :], PS[4][:, 0:B], DT / 6 / SCALE_V, RB3D[:, :], ALU.mult, ALU.add).then_inc(rk_yd, 1)
                dve.wait_ge(rk_yd, s)
                dve.wait_ge(rk_ys, s)
                TT(Y[:, :], Y[:, :], YD[:, :], ALU.add).then_inc(rk_y, 1)

            step(0, True)
            with dve.Fori(1, STEPS) as s:
                step(s, False)
            state(STEPS)
            dve.wait_ge(rk_ys, STEPS + 1)
            with dve.Fori(0, PAIRS) as i:
                for par in range(2):
                    TT(SQ[:, par], X[:, tile(i, par)], N[:, tile(i, par)], ALU.add).then_inc(o_s, 1)
                dve.wait_ge(o_tr, 2 * i + 2)


def kernel(**inputs):
    import numpy as np
    import concourse.bacc as bacc
    from concourse.bass_utils import run_bass_kernel_spmd

    f = {k: np.asarray(a) for k, a in inputs.items()}
    t = np.ascontiguousarray
    sel_e = np.zeros((NE, NE, 128), np.float32)
    for e in range(NE):
        sel_e[e, e] = 1
    arrays = {
        "x": f["x"].reshape(TOK, C),
        "wkq": np.concatenate([f["L0_conv_Wk"], f["L0_conv_Wq"]], 1),
        "wv": f["L0_conv_Wv"], "wr": f["L0_conv_Wr"],
        "bkq": np.concatenate([f["L0_conv_bk"], f["L0_conv_bq"]])[:, None],
        "bv": f["L0_conv_bv"][:, None], "br": f["L0_conv_br"][:, None],
        "wg": f["L0_ffn_Wg"],
        "w1": f["L0_ffn_W1"].transpose(1, 0, 2),
        "b1": f["L0_ffn_b1"].reshape(NE, MC, 128).transpose(2, 0, 1),
        "w2": f["L0_ffn_W2"].reshape(NE, MC, 128, C).transpose(2, 0, 1, 3),
        "b2": f["L0_ffn_b2"],
        "ck": f["L1_conv_kernel"].reshape(TAPS, 16, 128), "cb": f["L1_conv_bias"][:, None],
        "r1": f["L1_ffn_W1"].T,
        "r2": f["L1_ffn_W2"].T.reshape(MC, 128, HID).transpose(1, 0, 2).reshape(128, MC * HID),
        "r3": f["L1_ffn_W3"].T.reshape(MC, 128, C).transpose(1, 0, 2).reshape(128, MC * C),
        "r3n": f["L1_ffn_W3"],
        "rb1": f["L1_ffn_b1"].reshape(MC, 128).T, "rb2": f["L1_ffn_b2"].reshape(MC, 128).T, "rb3": f["L1_ffn_b3"][:, None],
        "ident": np.eye(128, dtype=np.float32),
        "iota": np.tile(np.arange(NE, dtype=np.float32), (128, 1)),
        "sel_e": sel_e,
    }
    nc = bacc.Bacc("TRN2", target_bir_lowering=False, num_devices=1)
    feed, args = {}, []
    for name, a in arrays.items():
        feed[f"in_{name}"] = t(a)
        args.append(nc.dram_tensor(f"in_{name}", a.shape, mybir.dt.from_np(a.dtype), kind="ExternalInput").ap())
    args.append(nc.dram_tensor("out", (TOK, C), F32, kind="ExternalOutput").ap())
    build(nc, *args)
    r = run_bass_kernel_spmd(nc, [feed], core_ids=[0])
    return r.results[0]["out"].reshape(B, HW, HW, C)
```

```python
from contextlib import ExitStack

import concourse.bass as bass
from concourse import mybir

F32 = mybir.dt.float32
F16 = mybir.dt.float16
BF16 = mybir.dt.bfloat16
ACT = mybir.ActivationFunctionType
ALU = mybir.AluOpType
AX = mybir.AxisListType

B, HW, C = 16, 16, 128
NPOS = HW * HW
TOK = B * NPOS
TILE = 512
IPT = TILE // NPOS
NT = TOK // TILE
PAIRS = NT // 2
QT = TILE // 128
DIM = 64
NE, HID = 8, 512
MC = HID // 128
TAPS = 9
PAD = HW + 2
STEPS = NPOS - 1
DT = 1.0 / STEPS
SUM = 4 * B
SCALE_V = 2.0 ** 8
SCALE_U = 2.0 ** 16
COEF = (DT / 2, DT, DT / 6)
COEF_OF = (0, 0, 1, 2)
LN_CONV, LN_TOK = 1e-6, 1e-5
GROUPS = NT * NE
SPG = 3
SCALE_M = 2.0 ** 8
START = 16
PE_ORDER = [(layer, m, k) for layer in range(2) for m in range(MC) for k in range(3)]
ACT_ORDER = {3 * m + 2 + full: (m, bool(full)) for m in range(MC) for full in range(2)}
ACC_SLOT, PIECES = 25, 4
S_STAT = 1 + SPG * GROUPS
S_CONV = S_STAT + 2 * NT
S_OUT = S_CONV + 5 * NT
OGB = 4
OG = B // OGB
S_PLAIN = S_OUT + OG
SCALE_C = 2.0 ** 8
SUB = 4
PT = SUB * B


def build(nc, scores, x, wkq, wv, wr, bkq, bv, br, wg, w1, b1, w2, b2, ck, cb, r1, r2, r3, r3n, rb1, rb2, rb3, ident,
          iota, sel_e, out):
    ctx = ExitStack()
    with ctx:
        def sb(name, shape, dt=F32):
            return ctx.enter_context(nc.sbuf_tensor(name, shape, dt))

        def sem(name):
            return ctx.enter_context(nc.semaphore(name))

        X = sb("X", [128, TOK])
        N = sb("N", [128, TOK])
        ONES = sb("ONES", [128, 128])
        ID = sb("ID", [128, 128])
        D4 = sb("D4", [128, 4, TILE])
        SQ4 = sb("SQ4", [128, 4, TILE])
        D, SD, SQ = D4[:, 0:2], D4[:, 2:4], SQ4[:, 0:2]
        WKQ = sb("WKQ", [128, 128])
        WV = sb("WV", [128, DIM])
        WR = sb("WR", [DIM, 128])
        BKQ = sb("BKQ", [128, 1])
        BV = sb("BV", [DIM, 1])
        BR = sb("BR", [128, 1])
        KQ = D
        V = sb("V", [DIM, 2, TILE])
        TK = SQ[:, :, :].rearrange("p a (q c) -> p a q c", q=QT)
        NM = sb("NM", [DIM, 2, 2 * IPT])
        SE = sb("SE", [DIM, 2, 2 * IPT])
        RP = sb("RP", [DIM, 2, IPT])
        GD = sb("GD", [DIM, 2, IPT, 128])
        OT = SD[0:DIM, :, :]
        WG = sb("WG", [128, NE])
        GP = sb("GP", [128, NT * QT, NE])
        GA = sb("GA", [128, NT * QT, NE])
        GO = sb("GO", [128, NT * QT, NE])
        GQ = sb("GQ", [128, NT * QT, NE])
        GR = sb("GR", [128, 8, NT * QT])
        IOTA = sb("IOTA", [128, NE])
        STC = sb("STC", [NE, PT])
        STF = sb("STF", [128, TOK])
        W2F = STF[:, :]
        ST = STF[0:NE, :]
        EPS = sb("EPS", [128, 2])
        SELE = sb("SELE", [NE, NE, 128])
        W1HL, W2HL = sb("W1HL", [128, 2 * NE * HID], F16), sb("W2HL", [128, 2 * NE * HID], F16)
        (W1H, W1L), (W2H, W2L) = (
            (w[:, 0:NE * HID].rearrange("p (e m n) -> p e m n", e=NE, m=MC),
             w[:, NE * HID:].rearrange("p (e m n) -> p e m n", e=NE, m=MC)) for w in (W1HL, W2HL))
        B1 = sb("B1", [128, NE * MC])
        B2 = sb("B2", [128, NE])
        B1E, B2E = sb("B1E", [128, MC]), sb("B2E", [128, 1])
        G = sb("G", [128, 4096])
        R2F = G[:, 0:2048]
        R3F, R3N = sb("R3F", [128, HID])[:, :], sb("R3N", [128, HID])[:, :]
        W13F = G[:, 2048:4096].rearrange("p (k n) -> p k n", k=MC)
        W13 = [W13F[:, k] for k in range(MC)]
        G16 = G[:, 0:2048].bitcast(F16).rearrange("p (h m n) -> p h m n", h=2, m=MC)
        GH, GL = G16[:, 0], G16[:, 1]
        GF = G[:, 2048:3072].rearrange("p (a n) -> p a n", a=2)
        TMP, SC = G[:, 3072:3584], G[:, 3584:4096]
        TMPC = TMP
        CK = sb("CK", [128, TAPS, 128])
        CB = sb("CB", [128, 1])
        NHL = sb("NHL", [128, TOK])
        W1F = NHL[:, :]
        NH = NHL[:, 0:TOK // 2].bitcast(F16)
        NL = NHL[:, TOK // 2:TOK].bitcast(F16)
        DD = W1HL[:, :].bitcast(F32)
        LV = W2HL[:, :].bitcast(F32)
        PADDED = IPT * PAD * PAD
        NPF, NPH, NPL = (a.rearrange("p (b y x) -> p b y x", b=IPT, y=PAD) for a in
                         (G[:, 0:PADDED], G[:, PADDED:3 * PADDED // 2].bitcast(F16),
                          G[:, 3 * PADDED // 2:2 * PADDED].bitcast(F16)))
        CKH, CKL = sb("CKH", [128, TAPS * 128], F16), sb("CKL", [128, TAPS * 128], F16)
        PNH, PNL = sb("PNH", [128, PT], F16), sb("PNL", [128, PT], F16)
        XP = sb("XP", [128, PT])
        X1 = sb("X1", [128, B])
        PGF = D[:, :, 0:MC * PT]
        PGH = SQ[:, 0, :].bitcast(F16)[:, 0:2 * MC * PT].rearrange("p (a n) -> p a n", a=2)
        PGL = SQ[:, 1, :].bitcast(F16)[:, 0:2 * MC * PT].rearrange("p (a n) -> p a n", a=2)
        PACC = SD[:, 0, :].rearrange("p (e n) -> p e n", e=NE)
        PMO = sb("PMO", [128, PT])
        RH2, RL2 = sb("RH2", [128, MC, MC, 128], F16), sb("RL2", [128, MC, MC, 128], F16)
        RH3, RL3 = sb("RH3", [128, MC, 128], F16), sb("RL3", [128, MC, 128], F16)
        RHU = sb("RHU", [128, 3, MC, MC, 128], F16)
        RLU = sb("RLU", [128, 3, MC, MC, 128], F16)
        IDU, IDV = sb("IDU", [128, 128], BF16), sb("IDV", [128, 128], BF16)
        RB1, RB2 = sb("RB1", [128, MC]), sb("RB2", [128, MC])
        RB3, RB3D = sb("RB3", [128, 1]), sb("RB3D", [128, 1])
        G0 = sb("G0", [128, MC])
        CW = sb("CW", [128, MC, B])
        CI = sb("CI", [128, 4, MC, 2, B], F16)
        R1K = sb("R1K", [128, HID])
        UI = sb("UI", [128, MC, 2, B], F16)
        AI = sb("AI", [128, MC, 2, B], F16)
        US = sb("US", [128, MC * B])
        DA = sb("DA", [128, MC * B])
        E = sb("E", [128, MC * B])
        AF = sb("AF", [128, MC, B])
        Y = sb("Y", [128, B])
        YD = sb("YD", [128, B])
        HA, HB = sb("HA", [128, MC, 2, B], F16), sb("HB", [128, MC, 2, B], F16)
        FA = sb("FA", [128, MC, B])
        FB = sb("FB", [128, 4, MC, B])
        HS, HT, HQ = (sb(n, [128, MC, B]) for n in ("HS", "HT", "HQ"))
        HSS = sb("HSS", [128, MC, 2, B], F16)
        XIN = N[:, :].rearrange("p (t q c) -> p t q c", t=NT, q=QT)
        YS = N[:, :].rearrange("p (b s) -> p b s", b=B)

        PSUM = ctx.enter_context(nc.psum_tensor("PSUM", [128, 8, 512], F32))
        PS = [PSUM[:, i] for i in range(8)]
        PA, PB = PS[0:2], PS[2:4]

        id_in, w_in, rk_in, mw_in, ck_in = (sem(k) for k in ("id_in", "w_in", "rk_in", "mw_in", "ck_in"))
        x_in = [sem(f"x_in{t}") for t in range(NT)]
        ck_zero, consts, w_hi, u_hi, w_lo = (sem(k) for k in ("ck_zero", "consts", "w_hi", "u_hi", "w_lo"))
        x_tr, x_c = sem("x_tr"), sem("x_c")
        ln_mean, ln_dev, ln_sq, ln_var, ln_log, ln_sd, ln_out = (
            sem("ln_" + k) for k in ("mean", "dev", "sq", "var", "log", "sd", "out"))
        at_pk, at_pv, at_kq, at_v, at_mk, at_mv, at_exp = (sem("at_" + k) for k in ("pk", "pv", "kq", "v", "mk", "mv", "exp"))
        at_tr, at_tk, at_prod, at_rp, at_gd, at_gds = (sem("at_" + k) for k in ("tr", "tk", "prod", "rp", "gd", "gds"))
        at_o, at_ot, at_y, at_x = (sem("at_" + k) for k in ("o", "ot", "y", "x"))
        g_l, g_v, g_e, g_ss, g_st, g_stc, g_sc = (sem("g_" + k) for k in ("l", "v", "e", "ss", "st", "stc", "sc"))
        pm_n, pm_s, pm_h, pm_g, pm_hi, pm_lo, pm_w, pm_e, pm_x, pm_ln, cv_p = (
            sem("pm_" + k) for k in ("n", "s", "h", "g", "hi", "lo", "w", "e", "x", "ln", "conv"))
        n_hi, n_lo, st_out, sc_in = (sem(k) for k in ("n_hi", "n_lo", "st_out", "sc_in"))
        mo_h, mo_hi, mo_f, mo_lo, mo_acc, mo_y, mo_x = (sem("mo_" + k) for k in ("h", "hi", "f", "lo", "acc", "y", "x"))
        b1e, b2e = sem("b1e"), sem("b2e")
        st_mean, st_dev, st_sq, st_var = (sem("st_" + k) for k in ("mean", "dev", "sq", "var"))
        cn_v, cn_s, cn_f, cn_h, cn_l, np_zero = (sem(k) for k in ("cn_v", "cn_s", "cn_f", "cn_h", "cn_l", "np_zero"))
        cv_p2, cv_y, cv_x = sem("cv_p2"), sem("cv_y"), sem("cv_x")
        rk_13, w13_out, rk_g0, rk_us = sem("rk_13"), sem("w13_out"), sem("rk_g0"), sem("rk_us")
        rk_p, rk_r, rk_hi, rk_f, rk_lo = (sem("rk_" + k) for k in ("p", "r", "hi", "f", "lo"))
        rk_u0, rk_ai, rk_uh, rk_u, rk_e = (sem("rk_" + k) for k in ("u0", "ai", "uh", "u", "e"))
        rk_hr, rk_hq, rk_hs, rk_k, rk_yd, rk_y, rk_ys = (sem("rk_" + k) for k in ("hr", "hq", "hs", "k", "yd", "y", "ys"))
        o_s, o_tr, o_c, o_out = (sem("o_" + k) for k in ("s", "tr", "c", "out"))
        block = ctx.enter_context(nc.Block())

        def tile(i, par):
            return bass.ts(2 * i + par, TILE)

        SMALL = [(WKQ[:, :], wkq), (WV[:, :], wv), (WR[:, :], wr), (BKQ[:, :], bkq),
                 (BV[:, :], bv), (BR[:, :], br), (WG[:, :], wg), (B1[:, :], b1), (B2[:, :], b2),
                 (CB[:, :], cb), (IOTA[:, :], iota), (SELE[:, :, :], sel_e)]
        ODE = [(RB1[:, :], rb1), (RB2[:, :], rb2), (RB3[:, :], rb3), (R1K[:, :], r1), (R2F, r2), (R3F, r3), (R3N, r3n)]
        flat_w, quarters = "p e m n -> p (e m n)", "p (q n) -> p q n"

        def quarter(q):
            parts = [(W1H.rearrange(flat_w), W1L.rearrange(flat_w), W1F, SCALE_M),
                     (W2H.rearrange(flat_w), W2L.rearrange(flat_w), W2F, SCALE_M),
                     (RH2[:].rearrange(flat_w), RL2[:].rearrange(flat_w), R2F, SCALE_V),
                     (RH3[:].rearrange("p m n -> p (m n)"), RL3[:].rearrange("p m n -> p (m n)"), R3F, SCALE_V),
                     (CKH[:, :], CKL[:, :], CK[:, :, :].rearrange("p t n -> p (t n)"), SCALE_C)]
            return [(*(a.rearrange(quarters, q=4)[:, bass.ds(q, 1)] for a in p[:3]), p[3]) for p in parts]

        def fused_quarter(q):
            return [(*(a[:, c, bass.ds(q, 1)].rearrange("p k m n -> p k (m n)") for a in (RHU, RLU)),
                     W13F[:, bass.ds(q, 1)], SCALE_U * COEF[c]) for c in range(3)]

        SCRATCH = scores[:, :].rearrange("(t e) n -> e t n", e=NE)

        def corner(a):
            return a.rearrange("p (b y x) -> p b y x", b=B, y=HW)[:, :, 0:2, 0:2]

        def inside(a):
            return a[:, :, 1:HW + 1, 1:HW + 1]

        def corners(a):
            return a.rearrange("p (b y x) -> p b y x", b=B, y=2)

        def count(s, j, layer, h):
            return 16 * s + 4 * j + 2 * layer + h + 1

        def work(i, slot, this=True, nxt=True):
            if this:
                yield i, slot + 8 * SPG - START
            if nxt and slot >= START:
                yield i + 1, slot - START

        def half_images(a, g, h):
            return a[:, bass.ts(g, OGB * NPOS)].rearrange("p (b h n) -> p b h n", b=OGB, h=2)[:, :, h]

        def half_rows(g, h):
            return out[bass.ts(g, OGB * NPOS), :].rearrange("(b h p) c -> p b h c", b=OGB, h=2)[:, :, h]

        FIRST_SUM = DD[:, 0:OGB * 128].rearrange("p (b n) -> p b n", b=OGB)

        def second_sum(g):
            return DD[:, bass.ts(g + 1, OGB * 128)].rearrange("p (b n) -> p b n", b=OGB)

        def out_blocks(g, h):
            return LV.rearrange("p (h n) -> p h n", h=2)[:, h, bass.ts(g, OGB * 128)]

        def moe_round(step, expert, i, this=True, nxt=True):
            def beside(slot):
                for g, own in work(i, slot, this, nxt):
                    expert(g, own)
            for r in range(SPG):
                if this or r == SPG - 1:
                    step(SPG * i + 1 + r, not this, beside, r)

        @block.sync
        def _(sp):
            sp.dma_start(ID[:, :], ident).then_inc(id_in, 16)
            for t in range(NT):
                sp.dma_start(XIN[:, t], x[t * TILE:(t + 1) * TILE, :].rearrange("(q p) c -> p q c", p=128)).then_inc(x_in[t], 16)
            for dst, src in SMALL:
                sp.dma_start(dst, src).then_inc(w_in, 16)
            for dst, src in ODE:
                sp.dma_start(dst, src).then_inc(rk_in, 16)
            sp.dma_start(W1F, w1).then_inc(mw_in, 16)
            sp.dma_start(W2F, w2).then_inc(mw_in, 16)
            sp.wait_ge(ck_zero, 1)
            for g in range(8):
                sp.dma_start(CK[16 * g:16 * g + 16, :, 16 * g:16 * g + 16],
                             ck[:, :, 16 * g:16 * g + 16].rearrange("t i o -> i t o")).then_inc(ck_in, 16)
            sp.wait_ge(g_sc, 8)
            sp.dma_start(SCRATCH, ST[:, :].rearrange("e (t n) -> e t n", t=NT)).then_inc(st_out, 16)
            sp.wait_ge(st_out, 16)
            sp.wait_ge(w_lo, 4)
            sp.dma_start(SC, scores[0:1, :].partition_broadcast(128)).then_inc(sc_in, 16)
            with sp.Fori(1, GROUPS) as g:
                sp.wait_ge(mo_y, PIECES * g)
                sp.dma_start(SC, scores[bass.ds(g, 1), :].partition_broadcast(128)).then_inc(sc_in, 16)
            with sp.Fori(0, OG) as g:
                sp.wait_ge(o_c, g + 1)
                sp.dma_start(half_rows(g, 0), out_blocks(g, 0).rearrange("p (b c) -> p b c", b=OGB)).then_inc(o_out, 16)
            for g in range(OG):
                sp.wait_ge(o_c, OG + g + 1)
                sp.dma_start(half_rows(g, 1), out_blocks(g, 1).rearrange("p (b c) -> p b c", b=OGB)).then_inc(o_out, 16)
            sp.wait_ge(o_out, 16 * 2 * OG)

        @block.gpsimd
        def _(gp):
            nc.gpsimd.memset(CK[:, :, :], 0.0).then_inc(ck_zero, 1)
            g = nc.gpsimd
            gp.wait_ge(rk_in, 16 * len(ODE))
            gp.wait_ge(mw_in, 32)
            gp.wait_ge(ck_in, 16 * 8)
            for q in range(4):
                for hi, _lo, src, scale in quarter(q):
                    t = g.tensor_scalar(hi, src, scale, None, ALU.mult)
                t.then_inc(w_hi, 1)
            gp.wait_ge(ln_out, 2 * NT)
            gp.wait_ge(w_lo, 4)
            g.tensor_copy(NH, N[:, :]).then_inc(n_hi, 1)
            gp.wait_ge(n_hi, 1)
            g.tensor_tensor(NL, N[:, :], NH, ALU.subtract).then_inc(n_lo, 1)
            gp.wait_ge(rk_y, 1)
            gp.wait_ge(n_lo, 1)
            nc.gpsimd.tensor_copy(YS[:, :, 0], Y[:, :]).then_inc(rk_ys, 1)

            def stage_sum(s):
                gp.wait_ge(rk_f, count(s, 3, 1, 1))
                g.tensor_tensor(HS[:, :, :], FB[:, 0], FB[:, 3], ALU.add).then_inc(rk_hr, 1)
                g.tensor_tensor(HT[:, :, :], FB[:, 1], FB[:, 2], ALU.add).then_inc(rk_hr, 1)
                gp.wait_ge(rk_hr, 2 * s + 2)
                g.tensor_tensor(HS[:, :, :], HS[:, :, :], HT[:, :, :], ALU.add).then_inc(rk_hq, 1)
                gp.wait_ge(rk_hq, 3 * s + 1)
                g.tensor_tensor(HQ[:, :, :], HS[:, :, :], HT[:, :, :], ALU.add).then_inc(rk_hq, 1)
                g.tensor_tensor(HSS[:, :, 0], HS[:, :, :], HT[:, :, :], ALU.add).then_inc(rk_hq, 1)
                gp.wait_ge(rk_hq, 3 * s + 3)
                g.tensor_tensor(HSS[:, :, 1], HQ[:, :, :], HSS[:, :, 0], ALU.subtract).then_inc(rk_hs, 1)

            def store(s):
                gp.wait_ge(rk_y, s + 1)
                g.tensor_copy(YS[:, :, bass.ds(s, 1)], Y[:, :].unsqueeze(2)).then_inc(rk_ys, 1)

            def gelu_low(i, m):
                gp.wait_ge(mo_f, MC * i + m + 1)
                g.tensor_tensor(GL[:, m], GF[:, m % 2], GH[:, m], ALU.subtract).then_inc(mo_lo, 1)

            def add(i):
                gp.wait_ge(mo_y, PIECES * (i + 1))
                tok = bass.ts(i // NE if isinstance(i, int) else gp.snap(i // NE), TILE)
                g.tensor_tensor(X[:, tok], X[:, tok], TMP, ALU.add).then_inc(mo_x, 1)

            def moe_round(i, nxt=True):
                s = SPG * i + 1
                gelu_low(i, 2)
                gelu_low(i, 3)
                store(s)
                stage_sum(s)
                store(s + 1)
                stage_sum(s + 1)
                if nxt:
                    gelu_low(i + 1, 0)
                add(i)
                store(s + 2)
                if nxt:
                    gelu_low(i + 1, 1)
                stage_sum(s + 2)

            gelu_low(0, 0)
            gelu_low(0, 1)
            stage_sum(0)
            with gp.Fori(0, GROUPS - 1) as i:
                moe_round(i)
            moe_round(GROUPS - 1, False)
            g.memset(NPH, 0.0).then_inc(np_zero, 1)
            g.memset(NPL, 0.0).then_inc(np_zero, 1)
            with gp.Fori(S_STAT, S_CONV) as s:
                store(s)
                stage_sum(s)
            with gp.Fori(0, NT) as t:
                gp.wait_ge(cn_h, t + 1)
                g.tensor_tensor(inside(NPL), inside(NPF), inside(NPH), ALU.subtract).then_inc(cn_l, 1)
                for r in range(5):
                    store(S_CONV + 5 * t + r)
                    stage_sum(S_CONV + 5 * t + r)
                gp.wait_ge(cv_y, t + 1)
                tok = bass.ts(t, TILE)
                g.tensor_tensor(X[:, tok], X[:, tok], TMP, ALU.add).then_inc(cv_x, 1)
            gp.wait_ge(cv_x, NT)
            gp.wait_ge(rk_ys, S_CONV)
            with gp.Fori(0, OG) as i:
                g.tensor_tensor(FIRST_SUM, half_images(X, i, 0), half_images(N, i, 0), ALU.add).then_inc(o_s, 1)
                store(S_OUT + i)
                stage_sum(S_OUT + i)
                gp.wait_ge(o_tr, i + 1)
            with gp.Fori(S_PLAIN, STEPS) as s:
                store(s)
                stage_sum(s)
            gp.wait_ge(rk_y, STEPS + 1)
            g.tensor_copy(YS[:, :, STEPS], Y[:, :]).then_inc(rk_ys, 1)

        @block.tensor
        def _(pe):
            mm = nc.tensor.matmul

            def layer_norm(p, beside):
                def mean(t):
                    mm(PS[t][:, :], ONES[:, :], X[:, bass.ts(t, TILE)], start=True, stop=True).then_inc(ln_mean, 1)

                for t in range(NT // 2):
                    mean(t)
                for t in range(NT):
                    pe.wait_ge(ln_sq, NT * p + t + 1)
                    mm(PS[t][:, :], ONES[:, :], SQ4[:, t % 4], start=True, stop=True).then_inc(ln_var, 1)
                    if t < NT // 2:
                        mean(NT // 2 + t)
                    if t % 4 == 3:
                        beside(t // 4)

            pe.wait_ge(id_in, 16)
            for t in range(NT):
                pe.wait_ge(x_in[t], 16)
                if t >= 2:
                    pe.wait_ge(x_c, t - 1)
                for q in range(QT):
                    tr = nc.tensor.transpose(PA[t % 2][:, bass.ts(q, 128)], XIN[:, t, q], ID[:, :])
                tr.then_inc(x_tr, 1)
            pe.wait_ge(x_c, NT)
            pe.wait_ge(consts, 1)

            def fuse(half):
                if half == 0:
                    pe.wait_ge(rk_in, 16 * len(ODE))
                    pe.wait_ge(ln_log, NT // 2)
                    for k in range(MC):
                        t = mm(PS[k][:, :], R3N[:, bass.ts(k, 128)], R1K[:, :], start=True, stop=True)
                    t.then_inc(rk_13, 1)

            layer_norm(0, fuse)
            pe.wait_ge(w_in, 16 * len(SMALL))

            def project(i):
                for par in range(2):
                    mm(PS[4 + par][:, :], WKQ[:, :], N[:, tile(i, par)], start=True, stop=True).then_inc(at_pk, 1)
                for par in range(2):
                    mm(PS[6 + par][0:DIM, :], WV[:, :], N[:, tile(i, par)], start=True, stop=True).then_inc(at_pv, 1)

            def attention_round(i, nxt=True):
                for par in range(2):
                    pe.wait_ge(at_exp, 2 * i + par + 1)
                    for q in range(QT):
                        t = nc.tensor.transpose(PA[par][:, bass.ts(q, 128)], KQ[:, par, bass.ts(q, 128)], ID[:, :])
                    t.then_inc(at_tr, 1)
                if nxt:
                    project(i + 1)
                for par in range(2):
                    pe.wait_ge(at_tk, 2 * i + par + 1)
                    for b in range(IPT):
                        for h in range(2):
                            t = mm(PB[par][0:DIM, bass.ts(b, DIM)], TK[:, par, 2 * b + h, 0:DIM],
                                   TK[:, par, 2 * b + h, DIM:128], start=(h == 0), stop=(h == 1))
                    t.then_inc(at_gd, 1)
                for par in range(2):
                    pe.wait_ge(at_gds, 2 * i + par + 1)
                    for b in range(IPT):
                        t = mm(PA[par][:, bass.ts(b, NPOS)], GD[:, par, b], V[:, par, bass.ts(b, NPOS)],
                               start=True, stop=True)
                    t.then_inc(at_o, 1)
                for par in range(2):
                    pe.wait_ge(at_ot, 2 * i + par + 1)
                    mm(PB[par][:, :], WR[:, :], OT[:, par], start=True, stop=True).then_inc(at_y, 1)
                pe.wait_ge(at_x, 2 * i + 2)

            pe.wait_ge(ln_out, NT)
            project(0)
            pe.wait_ge(w13_out, MC)
            with pe.Fori(0, PAIRS - 1) as i:
                attention_round(i)
            attention_round(PAIRS - 1, False)
            def logits(half):
                if half == 0:
                    pe.wait_ge(w_lo, 4)
                    pe.wait_ge(ln_log, NT + NT // 2)
                    for m in range(MC):
                        t = mm(PS[1][:, m:m + 1], R1K[:, bass.ts(m, 128)], RB3[:, :], start=(m == 0), stop=(m == MC - 1))
                    t.then_inc(rk_g0, 1)
                for t in range(NT // 2 * half, NT // 2 * (half + 1)):
                    pe.wait_ge(ln_out, NT + t + 1)
                    for n in range(QT * t, QT * (t + 1)):
                        r = mm(PS[0][:, bass.ts(n, NE)], N[:, bass.ts(n, 128)], WG[:, :], start=True, stop=True)
                if half == 1:
                    r.then_inc(g_l, 1)

            layer_norm(1, logits)

            def turn(half):
                for b in range(B):
                    t = nc.tensor.transpose(PS[4 + b // 4][0:NE, bass.ts(b % 4, 128)], GP[:, 2 * b + half], ID[:, :])
                    if b % 4 == 3:
                        t.then_inc(g_st, 1)

            pe.wait_ge(g_ss, 1)
            turn(0)
            pe.wait_ge(g_stc, 4)
            for e in range(NE):
                t = mm(PS[3][:, bass.ts(e, PT)], SELE[:, e], STC[:, :], start=True, stop=True)
            t.then_inc(pm_s, 1)
            pe.wait_ge(pm_n, 2)
            pe.wait_ge(w_lo, 4)

            def down(e):
                pe.wait_ge(pm_lo, e + 1)
                acc = PS[2][:, bass.ts(e, PT)]
                for m in range(MC):
                    c = bass.ts(m, PT)
                    mm(acc, W2H[:, e, m], PGH[:, e % 2, c], start=(m == 0), stop=False)
                    mm(acc, W2L[:, e, m], PGH[:, e % 2, c], start=False, stop=False)
                    t = mm(acc, W2H[:, e, m], PGL[:, e % 2, c], start=False, stop=(m == MC - 1))
                t.then_inc(pm_w, 1)

            for e in range(NE):
                if e >= 2:
                    pe.wait_ge(pm_g, e - 1)
                for m in range(MC):
                    h = PS[e % 2][:, bass.ts(m, PT)]
                    mm(h, W1H[:, e, m], PNH[:, :], start=True, stop=False)
                    mm(h, W1L[:, e, m], PNH[:, :], start=False, stop=False)
                    t = mm(h, W1H[:, e, m], PNL[:, :], start=False, stop=True)
                t.then_inc(pm_h, 1)
                if e:
                    down(e - 1)
            down(NE - 1)
            pe.wait_ge(g_sc, 4)
            turn(1)
            pe.wait_ge(pm_x, 1)
            mm(PA[0][:, 0:PT], ONES[:, :], XP[:, :], start=True, stop=True).then_inc(ln_mean, 1)
            pe.wait_ge(ln_sq, 2 * NT + 1)
            mm(PB[0][:, 0:PT], ONES[:, :], SQ[:, 0, 0:PT], start=True, stop=True).then_inc(ln_var, 1)
            pe.wait_ge(ck_in, 16 * 8)
            pe.wait_ge(pm_ln, 1)
            for n in range(SUB):
                y, x_ = n // 2, n % 2
                t = mm(PA[1][:, 0:B], CK[:, 3 * (y + 1) + x_ + 1], corners(PMO[:, :])[:, :, y, x_],
                       start=(n == 0), stop=(n == SUB - 1))
            t.then_inc(cv_p, 1)
            pe.wait_ge(pm_x, 2)
            mm(PA[0][:, 0:B], ONES[:, :], X1[:, :], start=True, stop=True).then_inc(ln_mean, 1)
            pe.wait_ge(ln_sq, 2 * NT + 2)
            mm(PB[0][:, 0:B], ONES[:, :], SQ[:, 0, 0:B], start=True, stop=True).then_inc(ln_var, 1)
            pe.wait_ge(rk_y, 1)
            for m in range(MC):
                t = mm(PS[3][:, bass.ts(m, B)], R1K[:, bass.ts(m, 128)], Y[:, :], start=(m == 0), stop=(m == MC - 1))
            t.then_inc(rk_u0, 1)
            PP, PK = (PS[0:2], PS[2:4]), PS[4]
            W = 2 * 2 * B

            def inject(lay, ident, what, start):
                for h in range(2):
                    mm(PP[lay][h][:, 0:W], ident[:, :], what[:, 2 * h:2 * h + 2], start=start, stop=False)

            def layer(s, j, lay, hi, lo, src, late):
                out = PP[1 - lay]

                def low(ks, ms):
                    for m in ms:
                        for k in ks:
                            mm(out[m // 2][:, 2 * B * (m % 2):2 * B * (m % 2) + B], lo[:, k, m], src[:, k, 0],
                               start=False, stop=False)

                def high(ks, ms, stop):
                    for m in ms:
                        for k in ks:
                            t = mm(out[m // 2][:, bass.ts(m % 2, 2 * B)], hi[:, k, m], src[:, k], start=False,
                                   stop=(stop and m % 2 == 1 and k == 3))
                    return t

                pe.wait_ge(rk_hi, count(s, j, lay, 0))
                low((0, 1), range(MC))
                pe.wait_ge(rk_hi, count(s, j, lay, 1))
                low((2, 3), (0, 1))
                late()
                pe.wait_ge(rk_lo, count(s, j, lay, 0))
                high((0, 1), range(MC), False)
                pe.wait_ge(rk_lo, count(s, j, lay, 1))
                high((2, 3), (0, 1), True).then_inc(rk_p, 1)
                low((2, 3), (2, 3))
                high((2, 3), (2, 3), True).then_inc(rk_p, 1)

            def state_product(part):
                for k in range(MC):
                    t = mm(PK[:, 0:B], (RL3 if part == 1 else RH3)[:, k], HSS[:, k, part // 2],
                           start=(part == 0 and k == 0), stop=(part == 2 and k == MC - 1))
                if part == 2:
                    t.then_inc(rk_k, 1)

            def expert(g, slot):
                first = isinstance(g, int) and g == 0
                if slot >= len(PE_ORDER):
                    return
                lay, m, k = PE_ORDER[slot]
                if slot == 7 and not first:
                    pe.wait_ge(mo_y, PIECES * g)
                if lay == 0:
                    if k == 0 and m >= 2:
                        pe.wait_ge(mo_f, MC * g + m - 1)
                    w = (W1L if k == 1 else W1H)
                    v = (NL if k == 2 else NH)[:, bass.ts(g // NE, TILE)]
                    out, start, stop = PS[5 + m % 2], k == 0, k == 2
                else:
                    if k == 0:
                        pe.wait_ge(mo_hi, MC * g + m + 1)
                    if k == 2:
                        pe.wait_ge(mo_lo, MC * g + m + 1)
                    w = (W2L if k == 1 else W2H)
                    v = (GL if k == 2 else GH)[:, m]
                    out, start, stop = PS[7], m == 0 and k == 0, m == MC - 1 and k == 2
                w = w.rearrange("p e m n -> p (e m) n")[:, bass.ds((g % NE) * MC + m, 1)].squeeze(1)
                t = mm(out[:, :], w, v, start=start, stop=stop)
                if k == 2 and lay == 0:
                    t.then_inc(mo_h, 1)
                elif stop:
                    t.then_inc(mo_acc, 1)

            def statistics(t, slot):
                if slot < 4:
                    r = mm(PS[5][:, bass.ts(slot, 128)], ONES[:, :], X[:, bass.ds(t * TILE + 128 * slot, 128)],
                           start=True, stop=True)
                    if slot == 3:
                        r.then_inc(st_mean, 1)
                q = slot - 11
                if 0 <= q < 4:
                    if q == 0:
                        pe.wait_ge(st_sq, t + 1)
                    r = mm(PS[6][:, bass.ts(q, 128)], ONES[:, :], SQ[:, 0, bass.ts(q, 128)], start=True, stop=True)
                    if q == 3:
                        r.then_inc(st_var, 1)

            def conv(t, slot):
                n = slot - 12
                if 0 <= n < 3 * TAPS:
                    k, tap = n // TAPS, n % TAPS
                    dy, dx = tap // 3, tap % 3
                    if n == 0:
                        pe.wait_ge(cn_h, t + 1)
                    if k == 2 and tap == 0:
                        pe.wait_ge(cn_l, t + 1)
                    r = mm(PS[5][:, :], (CKL if k == 1 else CKH)[:, bass.ts(tap, 128)],
                           (NPL if k == 2 else NPH)[:, :, dy:dy + HW, dx:dx + HW], start=(n == 0), stop=(n == 3 * TAPS - 1))
                    if n == 3 * TAPS - 1:
                        r.then_inc(cv_p2, 1)

            def step(s, first, beside=lambda slot: None, r=0):
                for j in range(4):
                    inject(1, IDV, CI[:, 3], True)
                    if j == 1 and not first:
                        pe.wait_ge(rk_hs, s)
                        state_product(0)
                    if j == 2 and not first:
                        state_product(2)
                    beside(8 * r + 2 * j)
                    layer(s, j, 0, RH2, RL2, HA, lambda: None)
                    beside(8 * r + 2 * j + 1)
                    pe.wait_ge(rk_u, 4 * s + j + 1)
                    inject(0, IDU, CI[:, COEF_OF[j]], True)
                    if j < 3:
                        inject(0, IDU, UI, False)
                    if j == 1 and not first:
                        state_product(1)

                    def late(j=j):
                        if j == 3:
                            pe.wait_ge(rk_ai, s + 2)
                            inject(0, IDU, AI, False)

                    layer(s, j, 1, RHU[:, COEF_OF[j]], RLU[:, COEF_OF[j]], HB, late)

            pe.wait_ge(rk_ai, 1)
            for h in range(2):
                mm(PP[0][h][:, 0:W], IDU[:, :], AI[:, 2 * h:2 * h + 2], start=True, stop=True).then_inc(rk_p, 1)
            pe.wait_ge(n_lo, 1)
            pe.wait_ge(g_sc, 8)
            moe_round(step, expert, -1, this=False)
            with pe.Fori(0, GROUPS - 1) as i:
                moe_round(step, expert, i)
            moe_round(step, expert, GROUPS - 1, nxt=False)
            pe.wait_ge(mo_x, GROUPS)
            with pe.Fori(0, NT) as t:
                for r in range(2):
                    step(S_STAT + 2 * t + r, False, lambda slot, t=t: statistics(t, slot), r)
            pe.wait_ge(np_zero, 2)
            with pe.Fori(0, NT) as t:
                for r in range(5):
                    step(S_CONV + 5 * t + r, False, lambda slot, t=t: conv(t, slot), r)
            def give(i, slot):
                q = slot - 2
                if 0 <= q < OGB:
                    if q == 0:
                        pe.wait_ge(o_s, i + 1)
                    r = nc.tensor.transpose(PS[5][:, bass.ts(q, 128)], FIRST_SUM[:, q], ID[:, :])
                    if q == OGB - 1:
                        r.then_inc(o_tr, 1)
                if slot == 7:
                    pe.wait_ge(o_c, i + 1)

            with pe.Fori(0, OG) as i:
                step(S_OUT + i, False, lambda slot, i=i: give(i, slot))
            with pe.Fori(S_PLAIN, STEPS) as s:
                step(s, False)
            pe.wait_ge(rk_hs, STEPS)
            for part in range(3):
                state_product(part)
            for i in range(OG):
                pe.wait_ge(o_s, OG + i + 1)
                for q in range(OGB):
                    t = nc.tensor.transpose(PS[i][:, bass.ts(q, 128)], second_sum(i)[:, q], ID[:, :])
                t.then_inc(o_tr, 1)

        @block.scalar
        def _(act):
            A = nc.scalar.activation

            def layer_norm(p, eps):
                for i in range(NT // 4):
                    for k in range(4):
                        act.wait_ge(ln_dev, NT * p + 4 * i + k + 1)
                        A(SQ4[:, k], D4[:, k], ACT.Square).then_inc(ln_sq, 1)
                    for k in range(4):
                        act.wait_ge(ln_var, NT * p + 4 * i + k + 1)
                        A(SQ4[:, k], PS[4 * i + k][:, :], ACT.Ln, bias=EPS[:, eps:eps + 1]).then_inc(ln_log, 1)
                    for k in range(4):
                        act.wait_ge(ln_log, NT * p + 4 * i + k + 1)
                        A(SQ4[:, k], SQ4[:, k], ACT.Exp, scale=-0.5).then_inc(ln_sd, 1)

            nc.scalar.preload_act_table_set("natural_log_exp_and_others")
            with act.Fori(0, PAIRS) as i:
                for par in range(2):
                    act.wait_ge(x_tr, 2 * i + par + 1)
                    nc.scalar.copy(X[:, tile(i, par)], PA[par][:, :]).then_inc(x_c, 1)
            act.wait_ge(consts, 1)
            act.wait_ge(w_in, 16 * len(SMALL))
            layer_norm(0, 0)
            act.wait_ge(rk_13, 1)
            for k in range(MC):
                nc.scalar.copy(W13[k], PS[k][:, :]).then_inc(w13_out, 1)

            def copy_kq(i):
                for par in range(2):
                    act.wait_ge(at_pk, 2 * i + par + 1)
                    A(KQ[:, par], PS[4 + par][:, :], ACT.Identity, bias=BKQ[:, :]).then_inc(at_kq, 1)

            def copy_v(i):
                for par in range(2):
                    act.wait_ge(at_pv, 2 * i + par + 1)
                    A(V[:, par], PS[6 + par][0:DIM, :], ACT.Identity, bias=BV[:, :]).then_inc(at_v, 1)

            def exps(i):
                for par in range(2):
                    act.wait_ge(at_mk, 2 * i + par + 1)
                    act.wait_ge(at_mv, 2 * i + par + 1)
                    act.wait_ge(at_v, 2 * i + par + 1)
                    for b in range(IPT):
                        A(KQ[0:DIM, par, bass.ts(b, NPOS)], KQ[0:DIM, par, bass.ts(b, NPOS)], ACT.Exp,
                          bias=NM[:, par, b:b + 1], accum_out=SE[:, par, b:b + 1])
                        t = A(V[:, par, bass.ts(b, NPOS)], V[:, par, bass.ts(b, NPOS)], ACT.Exp,
                              bias=NM[:, par, IPT + b:IPT + b + 1], accum_out=SE[:, par, IPT + b:IPT + b + 1])
                    t.then_inc(at_exp, 1)

            def attention_round(i, nxt=True):
                for par in range(2):
                    act.wait_ge(at_tr, 2 * i + par + 1)
                    nc.scalar.copy(TK[:, par].rearrange("p q c -> p (q c)"), PA[par][:, :]).then_inc(at_tk, 1)
                if nxt:
                    copy_kq(i + 1)
                for par in range(2):
                    act.wait_ge(at_o, 2 * i + par + 1)
                    nc.scalar.copy(OT[:, par], PA[par][0:DIM, :]).then_inc(at_ot, 1)
                if nxt:
                    copy_v(i + 1)
                    exps(i + 1)

            copy_kq(0)
            copy_v(0)
            exps(0)
            with act.Fori(0, PAIRS - 1) as i:
                attention_round(i)
            attention_round(PAIRS - 1, False)
            layer_norm(1, 1)
            act.wait_ge(g_v, 2)
            A(GP[:, :, :], GA[:, :, :], ACT.Exp).then_inc(g_e, 1)
            def turned(k, half):
                dst = ST[:, bass.ts(k, 4 * NPOS)].rearrange("e (b h n) -> e b h n", b=4, h=2)[:, :, half]
                nc.scalar.copy(dst, PS[4 + k][0:NE, :].rearrange("e (b n) -> e b n", b=4)).then_inc(g_sc, 1)

            for k in range(4):
                act.wait_ge(g_st, k + 1)
                nc.scalar.copy(STC[:, bass.ts(k, PT // 4)].rearrange("e (b y x) -> e b y x", b=4, y=2),
                               PS[4 + k][0:NE, :].rearrange("e (b y x) -> e b y x", b=4, x=HW)[:, :, 0:2, 0:2]).then_inc(g_stc, 1)
            for k in range(4):
                turned(k, 0)
            nc.scalar.preload_act_table_set("gelu_and_others")
            for e in range(NE):
                act.wait_ge(pm_h, e + 1)
                if e >= 2:
                    act.wait_ge(pm_lo, e - 1)
                for m in range(MC):
                    c = bass.ts(m, PT)
                    t = A(PGF[:, e % 2, c], PS[e % 2][:, c], ACT.Gelu, bias=B1[:, MC * e + m:MC * e + m + 1], scale=1.0 / SCALE_M)
                t.then_inc(pm_g, 1)
            nc.scalar.preload_act_table_set("natural_log_exp_and_others")
            for n, width in enumerate((PT, B)):
                act.wait_ge(ln_dev, 2 * NT + n + 1)
                A(SQ[:, 0, 0:width], D[:, 0, 0:width], ACT.Square).then_inc(ln_sq, 1)
                act.wait_ge(ln_var, 2 * NT + n + 1)
                A(SD[:, 0, 0:width], PB[0][:, 0:width], ACT.Ln, bias=EPS[:, n:n + 1]).then_inc(ln_log, 1)
                act.wait_ge(ln_log, 2 * NT + n + 1)
                A(SD[:, 0, 0:width], SD[:, 0, 0:width], ACT.Exp, scale=-0.5).then_inc(ln_sd, 1)
            for k in range(4):
                act.wait_ge(g_st, 4 + k + 1)
                turned(k, 1)
            nc.scalar.preload_act_table_set("gelu_and_others")

            def expert(g, slot):
                first = isinstance(g, int) and g == 0
                if slot in ACT_ORDER:
                    m, full = ACT_ORDER[slot]
                    if full:
                        if m >= 2:
                            act.wait_ge(mo_lo, MC * g + m - 1)
                    else:
                        act.wait_ge(mo_h, MC * g + m + 1)
                        if m == 0:
                            act.wait_ge(b1e, g + 1)
                            if not first:
                                act.wait_ge(mo_acc, g)
                    A(GF[:, m % 2] if full else GH[:, m], PS[5 + m % 2][:, :], ACT.Gelu,
                      bias=B1E[:, m:m + 1], scale=1.0 / SCALE_M).then_inc(mo_f if full else mo_hi, 1)

            def statistics(t, slot):
                if slot == 10:
                    act.wait_ge(st_dev, t + 1)
                    A(SQ[:, 0], DD[:, bass.ts(t, TILE)], ACT.Square).then_inc(st_sq, 1)
                if slot == 14:
                    act.wait_ge(st_var, t + 1)
                    nc.scalar.copy(LV[:, bass.ts(t, TILE)], PS[6][:, :]).then_inc(cn_v, 1)

            def conv(t, slot):
                if slot == 0:
                    A(SD[:, 0], LV[:, bass.ts(t, TILE)], ACT.Exp, scale=-0.5).then_inc(cn_s, 1)
                if slot == 7:
                    act.wait_ge(cn_f, t + 1)
                    nc.scalar.copy(inside(NPH), inside(NPF)).then_inc(cn_h, 1)
                if slot == 39:
                    act.wait_ge(cv_p2, t + 1)
                    A(TMPC, PS[5][:, :], ACT.Identity, bias=CB[:, :], scale=1.0 / SCALE_C).then_inc(cv_y, 1)

            def step(s, first, beside=lambda slot: None, r=0):
                for j in range(4):
                    for lay, hi, f, scale in ((0, HA, FA, SCALE_U), (1, HB, FB[:, j], SCALE_V)):
                        if j == 0 and lay == 1 and not first:
                            act.wait_ge(rk_hr, 2 * s)
                        for h in range(2):
                            act.wait_ge(rk_r, count(s, j, lay, h))
                            src = PSUM[:, 2 * lay + h, SUM:SUM + 2 * B].rearrange("p (m b) -> p m b", m=2)
                            A(hi[:, 2 * h:2 * h + 2, 0], src, ACT.Tanh, scale=1.0 / scale).then_inc(rk_hi, 1)
                            A(f[:, 2 * h:2 * h + 2], src, ACT.Tanh, scale=1.0 / scale).then_inc(rk_f, 1)
                        beside(8 * r + 2 * j + lay)

            act.wait_ge(w_lo, 4)
            moe_round(step, expert, -1, this=False)
            with act.Fori(0, GROUPS - 1) as i:
                moe_round(step, expert, i)
            moe_round(step, expert, GROUPS - 1, nxt=False)
            with act.Fori(0, NT) as t:
                for r in range(2):
                    step(S_STAT + 2 * t + r, False, lambda slot, t=t: statistics(t, slot), r)
            act.wait_ge(cn_v, NT)
            nc.scalar.preload_act_table_set("natural_log_exp_and_others")
            A(LV, LV, ACT.Ln, bias=EPS[:, 0:1]).then_inc(cn_v, 1)
            nc.scalar.preload_act_table_set("exp_and_others")
            act.wait_ge(cn_v, NT + 1)
            with act.Fori(0, NT) as t:
                for r in range(5):
                    step(S_CONV + 5 * t + r, False, lambda slot, t=t: conv(t, slot), r)
            def give(i, slot):
                if slot == 6:
                    act.wait_ge(o_tr, i + 1)
                    nc.scalar.copy(out_blocks(i, 0), PS[5][:, :]).then_inc(o_c, 1)

            with act.Fori(0, OG) as i:
                step(S_OUT + i, False, lambda slot, i=i: give(i, slot))
            with act.Fori(S_PLAIN, STEPS) as s:
                step(s, False)
            for i in range(OG):
                act.wait_ge(o_tr, OG + i + 1)
                nc.scalar.copy(out_blocks(i, 1), PS[i][:, :]).then_inc(o_c, 1)

        @block.vector
        def _(dve):
            v = nc.vector
            TT, TS, STT = v.tensor_tensor, v.tensor_scalar, v.scalar_tensor_tensor

            def layer_norm(p):
                for i in range(NT // 4):
                    for k in range(4):
                        dve.wait_ge(ln_mean, NT * p + 4 * i + k + 1)
                        TT(D4[:, k], X[:, bass.ts(4 * i + k, TILE)], PS[4 * i + k][:, :], ALU.subtract).then_inc(ln_dev, 1)
                    for k in range(4):
                        dve.wait_ge(ln_sd, NT * p + 4 * i + k + 1)
                        TT(N[:, bass.ts(4 * i + k, TILE)], D4[:, k], SQ4[:, k], ALU.mult).then_inc(ln_out, 1)
                    dve.wait_ge(ln_out, NT * p + 4 * i + 4)

            v.memset(EPS[:, 0:1], LN_CONV)
            v.memset(EPS[:, 1:2], LN_TOK)
            v.memset(GD[:, :, :, :], 0.0)
            v.memset(ONES[:, :], 1.0 / C).then_inc(consts, 1)
            dve.wait_ge(w_in, 16 * len(SMALL))
            layer_norm(0)
            def maxima(i, which):
                src, done, at_m = ((KQ, at_kq, at_mk), (V, at_v, at_mv))[which]
                for par in range(2):
                    dve.wait_ge(done, 2 * i + par + 1)
                    v.tensor_reduce(NM[:, par, bass.ts(which, IPT)], src[0:DIM, par].rearrange("p (b n) -> p b n", b=IPT),
                                    AX.X, ALU.max, negate=True).then_inc(at_m, 1)

            def attention_round(i, nxt=True):
                if nxt:
                    maxima(i + 1, 0)
                for par in range(2):
                    dve.wait_ge(at_rp, 2 * i + par + 1)
                    dve.wait_ge(at_gd, 2 * i + par + 1)
                    for b in range(IPT):
                        t = TS(GD[:, par, b, 0:DIM], PB[par][0:DIM, bass.ts(b, DIM)], RP[:, par, b:b + 1], None, ALU.mult)
                    t.then_inc(at_gds, 1)
                for hi, lo, src, scale in fused_quarter(i):
                    t = TS(hi, src, scale, None, ALU.mult)
                t.then_inc(u_hi, 1)
                if nxt:
                    maxima(i + 1, 1)
                    residual(i)
                    low_halves(i)
                    reciprocals(i + 1)
                else:
                    low_halves(i)
                    residual(i)

            def residual(i):
                for par in range(2):
                    dve.wait_ge(at_y, 2 * i + par + 1)
                    STT(X[:, tile(i, par)], PB[par][:, :], BR[:, :], X[:, tile(i, par)], ALU.add, ALU.add).then_inc(at_x, 1)

            def low_halves(i):
                dve.wait_ge(w_hi, i + 1)
                for hi, lo, src, scale in quarter(i):
                    STT(lo, src, scale, hi, ALU.mult, ALU.subtract)
                dve.wait_ge(u_hi, i + 1)
                for hi, lo, src, scale in fused_quarter(i):
                    t = STT(lo, src, scale, hi, ALU.mult, ALU.subtract)
                t.then_inc(w_lo, 1)

            def reciprocals(i):
                for par in range(2):
                    dve.wait_ge(at_exp, 2 * i + par + 1)
                    TT(RP[:, par], SE[:, par, 0:IPT], SE[:, par, IPT:2 * IPT], ALU.mult).then_inc(at_prod, 1)
                for par in range(2):
                    dve.wait_ge(at_prod, 2 * i + par + 1)
                    v.reciprocal(RP[:, par], RP[:, par]).then_inc(at_rp, 1)

            maxima(0, 0)
            maxima(0, 1)
            reciprocals(0)
            dve.wait_ge(w13_out, MC)
            with dve.Fori(0, PAIRS - 1) as i:
                attention_round(i)
            attention_round(PAIRS - 1, False)
            dve.wait_ge(at_x, NT)
            layer_norm(1)
            dve.wait_ge(rk_g0, 1)
            dve.wait_ge(rk_in, 16 * len(ODE))
            TS(IDU[:, :], ID[:, :], SCALE_U, None, ALU.mult)
            TS(IDV[:, :], ID[:, :], SCALE_V, None, ALU.mult)
            v.tensor_copy(B1E[:, :], B1[:, 0:MC]).then_inc(b1e, 1)
            TS(B2[:, :], B2[:, :], SCALE_M, None, ALU.mult)
            v.memset(YD[:, :], 0.0)
            TS(RB3D[:, :], RB3[:, :], DT, None, ALU.mult)
            v.tensor_copy(G0[:, :], PS[1][:, 0:MC]).then_inc(rk_us, 1)
            dve.wait_ge(rk_us, 1)
            v.tensor_copy(B2E[:, :], B2[:, 0:1]).then_inc(b2e, 1)
            for n in range(4):
                src = (G0 if n < 3 else RB2)[:, :].unsqueeze(2).to_broadcast([128, MC, B])
                TS(CW[:, :, :], src, COEF[n] if n < 3 else 1.0, None, ALU.mult).then_inc(rk_us, 1)
                dve.wait_ge(rk_us, 2 + 3 * n)
                v.tensor_copy(CI[:, n, :, 0], CW[:, :, :]).then_inc(rk_us, 1)
                dve.wait_ge(rk_us, 3 + 3 * n)
                TT(CI[:, n, :, 1], CW[:, :, :], CI[:, n, :, 0], ALU.subtract).then_inc(rk_us, 1)
                dve.wait_ge(rk_us, 4 + 3 * n)
            links = [0]

            def link(ins):
                links[0] += 1
                ins.then_inc(g_v, 1)
                dve.wait_ge(g_v, links[0])

            ALL = [128, NT * QT, NE]

            def wide(k):
                return GR[:, k].unsqueeze(2).to_broadcast(ALL)

            IO = IOTA[:, :].unsqueeze(1).to_broadcast(ALL)
            LOGITS = PS[0][:, 0:NT * QT * NE].rearrange("p (n e) -> p n e", e=NE)
            dve.wait_ge(g_l, 1)
            link(v.tensor_reduce(GR[:, 0], LOGITS, AX.X, ALU.max))
            link(TT(GA[:, :, :], LOGITS, wide(0), ALU.subtract))
            dve.wait_ge(g_e, 1)
            link(v.tensor_reduce(GR[:, 1], GP[:, :, :], AX.X, ALU.add))
            link(v.reciprocal(GR[:, 1], GR[:, 1]))
            link(TT(GP[:, :, :], GP[:, :, :], wide(1), ALU.mult))
            link(v.tensor_reduce(GR[:, 2], GP[:, :, :], AX.X, ALU.max))
            link(TT(GA[:, :, :], GP[:, :, :], wide(2), ALU.is_lt))
            link(STT(GA[:, :, :], GA[:, :, :], float(NE), IO, ALU.mult, ALU.add))
            link(v.tensor_reduce(GR[:, 3], GA[:, :, :], AX.X, ALU.min))
            link(TT(GO[:, :, :], IO, wide(3), ALU.is_equal))
            link(STT(GQ[:, :, :], GO[:, :, :], -2.0, GP[:, :, :], ALU.mult, ALU.add))
            link(v.tensor_reduce(GR[:, 4], GQ[:, :, :], AX.X, ALU.max))
            link(TT(GA[:, :, :], GQ[:, :, :], wide(4), ALU.is_lt))
            link(STT(GA[:, :, :], GA[:, :, :], float(NE), IO, ALU.mult, ALU.add))
            link(v.tensor_reduce(GR[:, 5], GA[:, :, :], AX.X, ALU.min))
            link(TT(GQ[:, :, :], IO, wide(5), ALU.is_equal))
            link(TT(GO[:, :, :], GO[:, :, :], GQ[:, :, :], ALU.add))
            link(STT(GR[:, 6], GR[:, 2], 1e-6, GR[:, 4], ALU.add, ALU.add))
            link(v.reciprocal(GR[:, 6], GR[:, 6]))
            link(TS(GR[:, 6], GR[:, 6], 1.0 / SCALE_M, None, ALU.mult))
            link(TT(GP[:, :, :], GP[:, :, :], GO[:, :, :], ALU.mult))
            TT(GP[:, :, :], GP[:, :, :], wide(6), ALU.mult).then_inc(g_ss, 1)
            v.tensor_copy(corners(PNH[:, :]), corner(N[:, :])).then_inc(pm_n, 1)
            dve.wait_ge(pm_n, 1)
            TT(corners(PNL[:, :]), corner(N[:, :]), corners(PNH[:, :]), ALU.subtract).then_inc(pm_n, 1)
            for e in range(NE):
                dve.wait_ge(pm_g, e + 1)
                if e >= 2:
                    dve.wait_ge(pm_w, e - 1)
                v.tensor_copy(PGH[:, e % 2], PGF[:, e % 2]).then_inc(pm_hi, 1)
                dve.wait_ge(pm_hi, e + 1)
                TT(PGL[:, e % 2], PGF[:, e % 2], PGH[:, e % 2], ALU.subtract).then_inc(pm_lo, 1)
            dve.wait_ge(pm_w, NE)
            TT(PACC, PS[2][:, :].rearrange("p (e n) -> p e n", e=NE), B2[:, :].unsqueeze(2).to_broadcast([128, NE, PT]),
               ALU.add).then_inc(pm_e, 1)
            dve.wait_ge(pm_e, 1)
            dve.wait_ge(pm_s, 1)
            TT(PACC, PACC, PS[3][:, :].rearrange("p (e n) -> p e n", e=NE), ALU.mult).then_inc(pm_e, 1)
            dve.wait_ge(pm_e, 2)
            v.tensor_reduce(PMO[:, :], PACC.rearrange("p e n -> p n e"), AX.X, ALU.add).then_inc(pm_e, 1)
            dve.wait_ge(pm_e, 3)
            TT(corners(XP[:, :]), corner(X[:, :]), corners(PMO[:, :]), ALU.add).then_inc(pm_x, 1)
            for n, (width, src, out) in enumerate(((PT, XP, PMO), (B, X1, Y))):
                dve.wait_ge(ln_mean, 2 * NT + n + 1)
                dve.wait_ge(pm_x, n + 1)
                TT(D[:, 0, 0:width], src[:, :], PA[0][:, 0:width], ALU.subtract).then_inc(ln_dev, 1)
                dve.wait_ge(ln_sd, 2 * NT + n + 1)
                TT(out[:, :], D[:, 0, 0:width], SD[:, 0, 0:width], ALU.mult).then_inc(pm_ln if n == 0 else rk_y, 1)
                if n == 0:
                    dve.wait_ge(cv_p, 1)
                    STT(X1[:, :], PA[1][:, 0:B], CB[:, :], corners(XP[:, :])[:, :, 0, 0], ALU.add, ALU.add).then_inc(pm_x, 1)
            dve.wait_ge(rk_u0, 1)
            TT(US[:, :].rearrange("p (m b) -> p m b", m=MC), PS[3][:, 0:MC * B].rearrange("p (m b) -> p m b", m=MC),
               RB1[:, :].unsqueeze(2).to_broadcast([128, MC, B]), ALU.add).then_inc(rk_us, 1)
            dve.wait_ge(rk_us, 14)
            US3 = US[:, :].rearrange("p (m b) -> p m b", m=MC)
            v.tensor_copy(AI[:, :, 0], US3).then_inc(rk_us, 1)
            dve.wait_ge(rk_us, 15)
            TT(AI[:, :, 1], US3, AI[:, :, 0], ALU.subtract).then_inc(rk_ai, 1)
            BOTH = PSUM[:, 0:2, SUM:SUM + 2 * B]

            def quad(a):
                if len(a.shape) == 2:
                    return a.rearrange("p (h m b) -> p h m b", h=2, m=2)
                if a.shape[1] == 2:
                    return a.rearrange("p h (m b) -> p h m b", m=2)
                return a.rearrange("p (h m) b -> p h m b", h=2)

            def two(a):
                return a[:, :].rearrange("p (h n) -> p h n", h=2)

            def expert(g, slot):
                last = isinstance(g, int) and g == GROUPS - 1
                if slot == 17 and not last:
                    dve.wait_ge(mo_f, MC * g + MC)
                    v.tensor_copy(B1E[:, :], B1[:, bass.ts((g + 1) % NE, MC)]).then_inc(b1e, 1)
                h = slot - ACC_SLOT
                if 0 <= h < PIECES:
                    if h == 0:
                        dve.wait_ge(b2e, g + 1)
                        dve.wait_ge(mo_acc, g + 1)
                        dve.wait_ge(sc_in, 16 * g + 16)
                    c = bass.ts(h, TILE // PIECES)
                    STT(TMP[:, c], PS[7][:, c], B2E[:, :], SC[:, c], ALU.add, ALU.mult).then_inc(mo_y, 1)
                if slot == 30 and not last:
                    dve.wait_ge(mo_y, PIECES * (g + 1))
                    dve.wait_ge(mo_x, g + 1)
                    v.tensor_copy(B2E[:, :], B2[:, bass.ds((g + 1) % NE, 1)]).then_inc(b2e, 1)

            def statistics(t, slot):
                if slot in (3, 4, 7, 9):
                    q = (3, 4, 7, 9).index(slot)
                    if q == 0:
                        dve.wait_ge(st_mean, t + 1)
                    tok = bass.ds(t * TILE + 128 * q, 128)
                    r = TT(DD[:, tok], X[:, tok], PS[5][:, bass.ts(q, 128)], ALU.subtract)
                    if q == 3:
                        r.then_inc(st_dev, 1)

            def conv(t, slot):
                if slot in (1, 3, 4, 6):
                    q = (1, 3, 4, 6).index(slot)
                    if q == 0:
                        dve.wait_ge(cn_s, t + 1)
                    b, y = q // 2, 8 * (q % 2)
                    src = [a.rearrange("p (y x) -> p y x", y=8) for a in
                           (DD[:, bass.ds(t * TILE + 128 * q, 128)], SD[:, 0, bass.ts(q, 128)])]
                    r = TT(NPF[:, b, 1 + y:9 + y, 1:HW + 1], src[0], src[1], ALU.mult)
                    if q == 3:
                        r.then_inc(cn_f, 1)

            def step(s, first, beside=lambda slot: None, r=0):
                for j in range(4):
                    for lay, hi, f in ((0, HA, FA), (1, HB, FB[:, j])):
                        for h in range(2):
                            bank = PSUM[:, 2 * lay + h]
                            dve.wait_ge(rk_p, count(s, j, lay, h))
                            v.tensor_reduce(bank[:, SUM:SUM + 2 * B].rearrange("p (m b) -> p m b", m=2),
                                            bank[:, 0:4 * B].rearrange("p (m c b) -> p m b c", m=2, c=2),
                                            AX.X, ALU.add).then_inc(rk_r, 1)
                        if lay == 1 and j == 3:
                            dve.wait_ge(rk_u, 4 * s + 4)
                            TT(AI[:, :, 1], AF[:, :, :], AI[:, :, 0], ALU.subtract).then_inc(rk_ai, 1)
                        for h in range(2):
                            dve.wait_ge(rk_f, count(s, j, lay, h))
                            sl = slice(2 * h, 2 * h + 2)
                            TT(hi[:, sl, 1], f[:, sl], hi[:, sl, 0], ALU.subtract).then_inc(rk_lo, 1)
                        if lay == 0:
                            if j == 0:
                                TS(quad(UI[:, :, 0]), quad(BOTH), 1.0 / SCALE_U, None, ALU.mult).then_inc(rk_uh, 1)
                                TS(two(US), BOTH, 1.0 / SCALE_U, None, ALU.mult)
                                dve.wait_ge(rk_uh, s + 1)
                                STT(quad(UI[:, :, 1]), quad(BOTH), 1.0 / SCALE_U, quad(UI[:, :, 0]), ALU.mult,
                                    ALU.subtract).then_inc(rk_u, 1)
                            elif j == 1:
                                STT(two(DA), two(US), -4.0 * SCALE_U, BOTH, ALU.mult, ALU.add).then_inc(rk_u, 1)
                            elif j == 2:
                                dve.wait_ge(rk_u, 4 * s + 2)
                                STT(two(DA), BOTH, 2.0, two(DA), ALU.mult, ALU.add).then_inc(rk_u, 1)
                            else:
                                dve.wait_ge(rk_e, s + 1)
                                STT(quad(AI[:, :, 0]), quad(BOTH), 1.0 / 3.0 / SCALE_U, quad(E[:, :]), ALU.mult, ALU.add)
                                STT(AF[:, :, :].rearrange("p (h m) b -> p h (m b)", h=2), BOTH, 1.0 / 3.0 / SCALE_U, two(E),
                                    ALU.mult, ALU.add).then_inc(rk_u, 1)
                        if lay == 1 and j == 2:
                            if not first:
                                state_increment(s)
                            STT(E[:, :], DA[:, :], 1.0 / 3.0 / SCALE_U, US[:, :], ALU.mult, ALU.add).then_inc(rk_e, 1)
                            if not first:
                                state(s)
                        beside(8 * r + 2 * j + lay)

            def state_increment(s):
                dve.wait_ge(rk_k, s)
                TS(YD[:, :], PS[4][:, 0:B], DT / 6 / SCALE_V, RB3D[:, :], ALU.mult, ALU.add).then_inc(rk_yd, 1)

            def state(s):
                dve.wait_ge(rk_yd, s)
                dve.wait_ge(rk_ys, s)
                TT(Y[:, :], Y[:, :], YD[:, :], ALU.add).then_inc(rk_y, 1)

            moe_round(step, expert, -1, this=False)
            with dve.Fori(0, GROUPS - 1) as i:
                moe_round(step, expert, i)
            moe_round(step, expert, GROUPS - 1, nxt=False)
            with dve.Fori(0, NT) as t:
                for r in range(2):
                    step(S_STAT + 2 * t + r, False, lambda slot, t=t: statistics(t, slot), r)
            with dve.Fori(0, NT) as t:
                for r in range(5):
                    step(S_CONV + 5 * t + r, False, lambda slot, t=t: conv(t, slot), r)
            with dve.Fori(S_OUT, STEPS) as s:
                step(s, False)
            state_increment(STEPS)
            state(STEPS)
            dve.wait_ge(cv_x, NT)
            dve.wait_ge(rk_ys, STEPS + 1)
            for i in range(OG):
                TT(second_sum(i), half_images(X, i, 1), half_images(N, i, 1), ALU.add).then_inc(o_s, 1)


def kernel(**inputs):
    import numpy as np
    import concourse.bacc as bacc
    from concourse.bass_utils import run_bass_kernel_spmd

    f = {k: np.asarray(a) for k, a in inputs.items()}
    t = np.ascontiguousarray
    sel_e = np.zeros((NE, NE, 128), np.float32)
    for e in range(NE):
        sel_e[e, e] = 1
    arrays = {
        "x": f["x"].reshape(TOK, C),
        "wkq": np.concatenate([f["L0_conv_Wk"], f["L0_conv_Wq"]], 1),
        "wv": f["L0_conv_Wv"], "wr": f["L0_conv_Wr"],
        "bkq": np.concatenate([f["L0_conv_bk"], f["L0_conv_bq"]])[:, None],
        "bv": f["L0_conv_bv"][:, None], "br": f["L0_conv_br"][:, None],
        "wg": f["L0_ffn_Wg"],
        "w1": f["L0_ffn_W1"].transpose(1, 0, 2).reshape(C, NE * HID),
        "b1": f["L0_ffn_b1"].reshape(NE * MC, 128).T,
        "w2": f["L0_ffn_W2"].reshape(NE * MC, 128, C).transpose(1, 0, 2).reshape(128, NE * MC * C),
        "b2": f["L0_ffn_b2"].T,
        "ck": f["L1_conv_kernel"].reshape(TAPS, 16, 128), "cb": f["L1_conv_bias"][:, None],
        "r1": f["L1_ffn_W1"].T,
        "r2": f["L1_ffn_W2"].T.reshape(MC, 128, HID).transpose(1, 0, 2).reshape(128, MC * HID),
        "r3": f["L1_ffn_W3"].T.reshape(MC, 128, C).transpose(1, 0, 2).reshape(128, MC * C),
        "r3n": f["L1_ffn_W3"],
        "rb1": f["L1_ffn_b1"].reshape(MC, 128).T, "rb2": f["L1_ffn_b2"].reshape(MC, 128).T, "rb3": f["L1_ffn_b3"][:, None],
        "ident": np.eye(128, dtype=np.float32),
        "iota": np.tile(np.arange(NE, dtype=np.float32), (128, 1)),
        "sel_e": sel_e,
    }
    nc = bacc.Bacc("TRN2", target_bir_lowering=False, num_devices=1)
    feed, args = {}, []
    for name, a in arrays.items():
        feed[f"in_{name}"] = t(a)
        args.append(nc.dram_tensor(f"in_{name}", a.shape, mybir.dt.from_np(a.dtype), kind="ExternalInput").ap())
    args.append(nc.dram_tensor("out", (TOK, C), F32, kind="ExternalOutput").ap())
    scores = nc.dram_tensor("scores", (GROUPS, TILE), F32).ap()
    build(nc, scores, *args)
    r = run_bass_kernel_spmd(nc, [feed], core_ids=[0])
    return r.results[0]["out"].reshape(B, HW, HW, C)
```
